# Optimizing a Trainium2 kernel written in Bass

```python
import numpy as np
import jax
import jax.numpy as jnp

def _softmax(x, axis=-1):
    return jax.nn.softmax(x, axis=axis)

def _gelu(x):
    return jax.nn.gelu(x, approximate=True)

def _silu(x):
    return jax.nn.silu(x)

def _sigmoid(x):
    return jax.nn.sigmoid(x)

def _layernorm(x, axis=-1, eps=1e-05):
    m = jnp.mean(x, axis=axis, keepdims=True)
    v = jnp.var(x, axis=axis, keepdims=True)
    return (x - m) / jnp.sqrt(v + eps)

def _scatter_add(tgt, idx, src, axis=0):
    return tgt.at[idx].add(src)

def _segment_sum(src, seg, n):
    return jax.ops.segment_sum(src, seg, n)
kernel_name = 'mk_flamingo_gated_d1_seqx_r2_16b317'

def setup_inputs(seed: int=0):
    np.random.seed(seed)
    _w = jnp.asarray

    def _rec_inputs():
        import jax
        import jax.numpy as jnp
        _rk = jax.random.key(seed)
        x = -0.0003929 + 0.9999 * jax.random.normal(jax.random.fold_in(_rk, 1), (16, 256, 1024), jnp.float32)
        _lenS = 256 - jax.random.randint(jax.random.fold_in(_rk, 7), (16,), 0, max(1, 256 // 4) + 1, jnp.int32)
        _lenS2 = 256 - jax.random.randint(jax.random.fold_in(_rk, 8), (16,), 0, max(1, 256 // 4) + 1, jnp.int32)
        _ctx_1024P = jax.random.normal(jax.random.fold_in(_rk, 11), (16, 16, 512), jnp.float32)
        _ctx_1024c = jax.random.dirichlet(jax.random.fold_in(_rk, 511), 0.3 * jnp.ones((16,), jnp.float32), (16, 256))
        _ctx_1024t = jnp.einsum('bsk,bkd->bsd', _ctx_1024c, _ctx_1024P)
        _ctx_1024t = _ctx_1024t * jax.lax.rsqrt(jnp.mean(jnp.square(_ctx_1024t)) + 1e-12) * 0.953939
        ctx_1024 = 4.13588e-05 + 0.999923 * (_ctx_1024t + 0.3 * jax.random.normal(jax.random.fold_in(_rk, 611), (16, 256, 512), jnp.float32))
        _validS = jnp.arange(256)[None, :] < _lenS[:, None]
        _validS2 = jnp.arange(256)[None, :] < _lenS2[:, None]
        _causal = jnp.tril(jnp.ones((256, 256), dtype=bool))
        mask_Bx1x2048_ff1 = jnp.where(jnp.ones((16, 1, 1024), dtype=bool), 1.0, 0.0).astype(jnp.float32)
        mask_Bx1x1024_ff1 = jnp.where(jnp.ones((16, 1, 512), dtype=bool), 1.0, 0.0).astype(jnp.float32)
        _g = jax.random.normal(jax.random.fold_in(_rk, 9001), (2, 1), jnp.float32)
        _g = jnp.sign(_g) * jnp.maximum(jnp.abs(_g), 1.0) + (_g == 0) * 1.0
        g_xattn = _g[0]
        g_ffn = _g[1]
        return (x, ctx_1024, mask_Bx1x2048_ff1, mask_Bx1x1024_ff1, g_xattn, g_ffn)
    x, ctx_1024, mask_Bx1x2048_ff1, mask_Bx1x1024_ff1, g_xattn, g_ffn = _rec_inputs()

    def _L0_xattn_setup():
        import jax, jax.numpy as jnp
        import numpy as np
        B, E, COND, TX, TY, H = (16, 256, 256, 1024, 512, 8)
        D = E // H
        SCALE = float(E // H ** 0.5)
        EPS = 1e-05

        def _ws(w):
            m = w.mean(axis=1, keepdims=True)
            v = w.var(axis=1, keepdims=True)
            return (w - m) * jax.lax.rsqrt(v + EPS)

        def _conv(x, w, b, mask):
            out = jnp.einsum('oc,bct->bot', _ws(w), x) + b[None, :, None]
            return out * mask
        key = jax.random.key(seed)
        ks = jax.random.split(key, 12)
        inp = {'x': jax.random.normal(ks[0], (B, E, TX), jnp.float32), 'y': jax.random.normal(ks[1], (B, COND, TY), jnp.float32), 'mask': jnp.ones((B, 1, TX), jnp.float32), 'mask_cond': jnp.ones((B, 1, TY), jnp.float32), 'wq': jax.random.normal(ks[2], (E, COND), jnp.float32) * 0.02, 'bq': jnp.zeros((E,), jnp.float32), 'wk': jax.random.normal(ks[3], (E, COND), jnp.float32) * 0.02, 'bk': jnp.zeros((E,), jnp.float32), 'wv': jax.random.normal(ks[4], (E, E), jnp.float32) * 0.02, 'bv': jnp.zeros((E,), jnp.float32), 'wo': jax.random.normal(ks[5], (E, E), jnp.float32) * 0.02, 'bo': jnp.zeros((E,), jnp.float32), 'gamma': jnp.ones((E,), jnp.float32), 'beta': jnp.zeros((E,), jnp.float32)}
        return inp
    _L0_xattn_all = _L0_xattn_setup()
    _L0_xattn_in = {k: v for k, v in _L0_xattn_all.items() if k in ('wq', 'bq', 'wk', 'bk', 'wv', 'bv', 'wo', 'bo', 'gamma', 'beta')}
    del _L0_xattn_all

    def _L0_ffn_setup():
        import jax, jax.numpy as jnp
        import numpy as np
        TOP_K = 2
        key = jax.random.key(seed)
        ks = jax.random.split(key, 5)
        B, S, D, INTER, E = (4, 1024, 1024, 1024, 8)
        x = jax.random.normal(ks[0], (B, S, D), dtype=jnp.float32)
        w1 = jax.random.normal(ks[1], (INTER, D), dtype=jnp.float32) * (1.0 / np.sqrt(D))
        w3 = jax.random.normal(ks[2], (INTER, INTER), dtype=jnp.float32) * (1.0 / np.sqrt(INTER))
        w2 = jax.random.normal(ks[3], (D, INTER), dtype=jnp.float32) * (1.0 / np.sqrt(INTER))
        wr = jax.random.normal(ks[4], (E, D), dtype=jnp.float32) * (1.0 / np.sqrt(D))
        return {'x': x, 'w1': w1, 'w3': w3, 'w2': w2, 'wr': wr}
    _L0_ffn_all = _L0_ffn_setup()
    _L0_ffn_in = {k: v for k, v in _L0_ffn_all.items() if k in ('w1', 'w3', 'w2', 'wr')}
    del _L0_ffn_all
    return {'x': x, 'ctx_1024': ctx_1024, 'mask_Bx1x2048_ff1': mask_Bx1x2048_ff1, 'mask_Bx1x1024_ff1': mask_Bx1x1024_ff1, 'g_xattn': g_xattn, 'g_ffn': g_ffn, 'L0_xattn_wq': _L0_xattn_in['wq'], 'L0_xattn_bq': _L0_xattn_in['bq'], 'L0_xattn_wk': _L0_xattn_in['wk'], 'L0_xattn_bk': _L0_xattn_in['bk'], 'L0_xattn_wv': _L0_xattn_in['wv'], 'L0_xattn_bv': _L0_xattn_in['bv'], 'L0_xattn_wo': _L0_xattn_in['wo'], 'L0_xattn_bo': _L0_xattn_in['bo'], 'L0_xattn_gamma': _L0_xattn_in['gamma'], 'L0_xattn_beta': _L0_xattn_in['beta'], 'L0_ffn_w1': _L0_ffn_in['w1'], 'L0_ffn_w3': _L0_ffn_in['w3'], 'L0_ffn_w2': _L0_ffn_in['w2'], 'L0_ffn_wr': _L0_ffn_in['wr']}

def reference(x, ctx_1024, mask_Bx1x2048_ff1, mask_Bx1x1024_ff1, g_xattn, g_ffn, L0_xattn_wq, L0_xattn_bq, L0_xattn_wk, L0_xattn_bk, L0_xattn_wv, L0_xattn_bv, L0_xattn_wo, L0_xattn_bo, L0_xattn_gamma, L0_xattn_beta, L0_ffn_w1, L0_ffn_w3, L0_ffn_w2, L0_ffn_wr):
    import jax
    import jax.numpy as jnp

    def _L0_xattn_ref(x, y, mask, mask_cond, wq, bq, wk, bk, wv, bv, wo, bo, gamma, beta):
        import jax, jax.numpy as jnp
        import numpy as np
        B, E, COND, TX, TY, H = (16, 256, 256, 1024, 512, 8)
        D = E // H
        SCALE = float(E // H ** 0.5)
        EPS = 1e-05

        def _ws(w):
            m = w.mean(axis=1, keepdims=True)
            v = w.var(axis=1, keepdims=True)
            return (w - m) * jax.lax.rsqrt(v + EPS)

        def _conv(x, w, b, mask):
            out = jnp.einsum('oc,bct->bot', _ws(w), x) + b[None, :, None]
            return out * mask
        q = _conv(y, wq, bq, mask_cond)
        k = _conv(y, wk, bk, mask_cond)
        v = _conv(x, wv, bv, mask)
        split = lambda t: t.reshape(t.shape[0], H, D, t.shape[-1])
        q, k, v = (split(q), split(k), split(v))
        scores = jax.nn.softmax(jnp.einsum('bhdt,bhet->bhde', q, k) / SCALE, axis=-1)
        out = jnp.einsum('bhde,bhet->bhdt', scores, v)
        out = out.reshape(out.shape[0], E, -1)
        out = _conv(out, wo, bo, mask) + x
        mu = out.mean(axis=1, keepdims=True)
        var = out.var(axis=1, keepdims=True)
        out = (out - mu) * jax.lax.rsqrt(var + EPS) * gamma[None, :, None] + beta[None, :, None]
        return out * mask

    def _L0_ffn_ref(x, w1, w3, w2, wr):
        import jax, jax.numpy as jnp
        import numpy as np
        TOP_K = 2
        B, S, D = x.shape
        xr = x.reshape(-1, D)
        route_probs = jax.nn.softmax(xr @ wr.T, axis=-1)
        routes_k, indices_k = jax.lax.top_k(route_probs, TOP_K)
        gates = routes_k / jnp.sum(routes_k, axis=-1, keepdims=True)
        h = jax.nn.silu(xr @ w1.T)
        h = jax.nn.silu(h @ w3.T)
        h = h @ w2.T
        out = jnp.zeros_like(xr)
        for k in range(TOP_K):
            out = out.at[indices_k[:, k]].add(gates[:, k:k + 1] * h)
        return out.reshape(B, S, D)
    x = x + jnp.tanh(g_xattn[0]) * _L0_xattn_ref(_layernorm(x, axis=-1), ctx_1024, mask_Bx1x2048_ff1, mask_Bx1x1024_ff1, L0_xattn_wq, L0_xattn_bq, L0_xattn_wk, L0_xattn_bk, L0_xattn_wv, L0_xattn_bv, L0_xattn_wo, L0_xattn_bo, L0_xattn_gamma, L0_xattn_beta)
    x = x + jnp.tanh(g_ffn[0]) * _L0_ffn_ref(_layernorm(x, axis=-1), L0_ffn_w1, L0_ffn_w3, L0_ffn_w2, L0_ffn_wr)
    return x

_drawn_inputs = setup_inputs


def setup_inputs(seed=0):
    import zlib

    import numpy as np

    out = dict(_drawn_inputs(seed))
    spreads = {'L0_xattn_bq': (0.0, 0.8),
     'L0_xattn_bk': (0.0, 0.8),
     'L0_xattn_bv': (0.0, 0.8),
     'L0_xattn_bo': (0.0, 0.8),
     'L0_xattn_gamma': (1.0, 0.2),
     'L0_xattn_beta': (0.0, 0.399)}
    factors = {}
    for name, (base, spread) in spreads.items():
        noise = np.random.default_rng([zlib.crc32(name.encode()), seed]).standard_normal(out[name].shape)
        drawn = base * np.exp(spread * noise) if base else spread * noise
        out[name] = jnp.asarray(drawn.astype(out[name].dtype))
    for name, factor in factors.items():
        out[name] = (out[name] * factor).astype(out[name].dtype)
    return out
```

```python
from contextlib import ExitStack

import concourse.bass as bass
from concourse import mybir

ALU = mybir.AluOpType
ACT = mybir.ActivationFunctionType
AX = mybir.AxisListType
F32 = mybir.dt.float32
F16 = mybir.dt.float16
I32 = mybir.dt.int32
U32 = mybir.dt.uint32
RMAX = bass.bass_isa.ReduceOp.max

P = 128
NB = 16
S = 256
T = 1024
TC = 512
HD = 32
NE = 8
CH = S // P
TT = T // P
CT = TC // P
PAIRS = NB // 2
TOK = 2 * S
FT = T // P
KT = TOK // P
GROUPS = FT + 2 * KT
SLOTS = GROUPS
EPS = 1e-5
SCORE = 1.0 / float(S // 8 ** 0.5)
XS = 1024.0
MS = 8.0
SMALL = 16 * 15
H1S = 2.0 ** -21
H2S = 2.0 ** -26


def build(nc, a, out):
    ctx = ExitStack()

    def sb(name, shape, dt=F32):
        return ctx.enter_context(nc.sbuf_tensor(name, shape, dt))

    def sem(name):
        return ctx.enter_context(nc.semaphore(name))

    def need(eng, s, count):
        if isinstance(count, int) and count <= 0:
            return
        eng.wait_ge(s, count)

    with ctx:
        w1_hi = sb("w1_hi", [P, FT, T], F16)
        w1_lo = sb("w1_lo", [P, FT, T], F16)
        w3_hi = sb("w3_hi", [P, FT, T], F16)
        w3_lo = sb("w3_lo", [P, FT, T], F16)
        stage = sb("stage", [P, 4 * 2048], F32)
        half = stage[:, :].bitcast(F16)
        xt_hi = half[:, 0:4096].rearrange("p (t n) -> p t n", t=TT)
        xt_lo = half[:, 4096:8192].rearrange("p (t n) -> p t n", t=TT)
        h1_hi = half[:, 8192:12288].rearrange("p (t n) -> p t n", t=FT)
        h1_lo = half[:, 12288:16384].rearrange("p (t n) -> p t n", t=FT)
        wst = stage[:, :].rearrange("p (t n) -> p t n", t=FT)
        xbuf = sb("xbuf", [P, 2, 2, CH, T], F32)
        xa = [xbuf[:, 0, b] for b in range(2)]
        xs = [xbuf[:, 1, b] for b in range(2)]
        w2st = xbuf[:, :, :, :, :].rearrange("p a b c t -> p (a b c) t")
        x_hi = sb("x_hi", [P, 2, CH, T], F16)
        x_lo = sb("x_lo", [P, 2, CH, T], F16)
        ya = sb("ya", [P, CH, TC])
        ub = sb("ub", [P, 2, 2048])
        qk = [ub[:, b, :].rearrange("p (t n) -> p t n", t=CT) for b in range(2)]
        u = [ub[:, b, :].rearrange("p (t n) -> p t n", t=TT) for b in range(2)]
        mrow = sb("mrow", [P, T])
        mtmp = sb("mtmp", [P, TC])
        act_t = sb("act_t", [P, 2, TOK])
        h2_hi = sb("h2_hi", [P, 2, TOK], F16)
        h2_lo = sb("h2_lo", [P, 2, TOK], F16)
        sblk = sb("sblk", [P, 2, CH, P])
        t1 = sb("t1", [P, CH, S])
        m_hi = sb("m_hi", [P, 2, CH, S], F16)
        m_lo = sb("m_lo", [P, 2, CH, S], F16)
        cb = sb("cb", [P, 2, S])
        bo_b = sb("bo_b", [P, S])
        qkb_b = sb("qkb_b", [P, 2 * S])
        wqk = sb("wqk", [P, CH, 2 * S])
        wo_t = sb("wo_t", [P, CH, S])
        wv_n = sb("wv_n", [P, CH, S])
        bv_b = sb("bv_b", [P, CH, P])
        ea = sb("ea", [P, S])
        eb = sb("eb", [P, S])
        wr_t = sb("wr_t", [P, FT, 2 * NE], F16)
        acc = sb("acc", [P, FT, 2 * NE])
        ident = sb("ident", [P, P])
        mtab = sb("mtab", [P, PAIRS, 56])
        mcur = sb("mcur", [P, 56])
        m1c = mcur[:, 0:16].rearrange("p (b t) -> p b t", b=2)
        m2c = mcur[:, 16:32].rearrange("p (b t) -> p b t", b=2)
        m2s = mcur[:, 32:48].rearrange("p (b t) -> p b t", b=2)
        mcc = mcur[:, 48:56].rearrange("p (b t) -> p b t", b=2)
        minus = sb("minus", [P, 8])
        nhalf = sb("nhalf", [P, 8])
        bst = sb("bst", [P, 8, 6])
        bst2 = sb("bst2", [P, 8, 6])
        mv = sb("mv", [P, 2, 2])
        mv2 = sb("mv2", [P, 2, 2])
        mvc = sb("mvc", [P, 8, 2])
        co = sb("co", [P, 4, 2])
        co2 = sb("co2", [P, 4, 2])
        coc = sb("coc", [P, 5, 8])
        dg = sb("dg", [P, CH, HD])
        dr = sb("dr", [P, 3, CH])
        gcol = sb("gcol", [P, 2, CH])
        tg = sb("tg", [P, 2])
        sc = sb("sc", [P, 3, 4])
        fs = sb("fs", [P, 4])
        lg = sb("lg", [P, KT, 2 * NE])
        lgs = sb("lgs", [P, KT, NE])
        top = sb("top", [P, KT, 8])
        topi = sb("topi", [P, KT, 8], U32)
        topf = sb("topf", [P, KT, 2])
        spare = sb("spare", [P, 1])
        gd = sb("gd", [P, 4, KT])
        iot = sb("iot", [P, NE])
        e1t = sb("e1t", [P, KT, NE])
        e2t = sb("e2t", [P, KT, NE])
        gts = sb("gts", [P, KT, 2 * NE], F16)
        acs = sb("acs", [P, FT, NE])
        wrs = x_hi[0:NE, 0].rearrange("p c t -> p (c t)").bitcast(F32)
        out8 = x_lo[0:NE, 0].rearrange("p c t -> p (c t)").bitcast(F32)

        bank = [ctx.enter_context(nc.psum_tensor(f"bank{n}", [P, 512], F32)) for n in range(8)]
        att = bank[0:4]
        fbk = bank[4:6]
        rbk, abk = bank[6], bank[7]

        x_in = [sem(f"x_in{b}") for b in range(2)]
        out_done = [sem(f"out_done{b}") for b in range(2)]
        names = """y_in mrow_in w1_in w3_in small_in
            ident_set s_zero sc_zero w_max w_all w_clamp w_bits w_scale w_tr w_hi w_lo wr_tr wr_hi wr_lo
            ws_stat ws_mv ws_var ws_rstd ws_coef ws_norm ws_tr ws_copy
            mask_tr mask_copy mask_sq tg_set gcol_set bias_set fs_part fs_set
            mcur_set ln1_stat ln1_mv ln1_var ln1_rstd ln1_coef xs_ready xhi_ready xlo_ready mtmp_step xpre_ready
            qk_mm qk_evac q_ready sc_mm sm_copy sm_max sm_sub sm_exp sm_sum sm_rec s_ready
            t1_mm t1_evac mt_mm mt_hi mt_lo cb_mm cb_evac
            e_mm e_bo e_cb u_ready u_stat cn_mv cn_var cn_rstd cn_mask cn_coef v_ready
            f_mm x2_ready ln2_stat ln2_mv ln2_var ln2_rstd ln2_coef xs2_ready g_mm xt_hi_set xt_lo_set
            z_mm th_ready z_used h_hi h_lo acc_mm acc_ready
            rt_mm rt_copy rt_sum rt_max rt_idx rt_idx2 rt_gap rt_exp rt_den rt_g1 rt_g2 rt_eq rt_sel rt_gate
            gates_hi gates_ready
            w2_in w2_tr w2_copy acs_set fin_mm fin_ready row_in fin_out""".split()
        sm = {n: sem(n) for n in names}

        xd = a["x"].rearrange("q (h p) t -> q p h t", p=P)
        yd = a["ctx"].rearrange("q (h p) t -> q p h t", p=P)
        od = out.rearrange("q (h p) t -> q p h t", p=P)
        wn = ub[:, 0, :].rearrange("p (w n) -> p w n", w=8)
        ws = ub[:, 1, :].rearrange("p (w n) -> p w n", w=8)
        msk = act_t[:, 0, 0:P]
        mskc = act_t[0:NB * CT, 0, P:2 * P]
        vrow = act_t[0:6, 0, 2 * P:3 * P]
        vcol = act_t[:, 1, 0:6]
        graw = act_t[:, 1, 8:10]
        w2t = [w1_hi[:, :, :].rearrange("p t n -> p (t n)").bitcast(F32).rearrange("p (t n) -> p t n", t=4),
               w1_lo[:, :, :].rearrange("p t n -> p (t n)").bitcast(F32).rearrange("p (t n) -> p t n", t=4)]

        block = ctx.enter_context(nc.Block())

        @block.sync
        def _(sp):
            sp.dma_start(wst, a["w1"].rearrange("(f p) d -> p f d", p=P)).then_inc(sm["w1_in"], 16)

            def loads(j):
                for b in range(2):
                    q = 2 * j + b
                    need(sp, out_done[b], 16 * j)
                    need(sp, sm["xs2_ready"], q - 1)
                    sp.dma_start(xa[b], xd[q]).then_inc(x_in[b], 16)
                for b in range(2):
                    q = 2 * j + b
                    need(sp, sm["qk_mm"], CT * q)
                    sp.dma_start(ya[:, :, :], yd[q]).then_inc(sm["y_in"], 16)
                    need(sp, sm["xpre_ready"], q)
                    sp.dma_start(mrow[:, :], a["mask"][q, 0, :].partition_broadcast(P)).then_inc(sm["mrow_in"], 16)

            def stores(j):
                for b in range(2):
                    q = 2 * j + b
                    need(sp, sm["x2_ready"], 4 * q + 4)
                    sp.dma_start(od[q], xa[b]).then_inc(out_done[b], 16)

            loads(0)
            stores(0)
            with sp.Fori(0, PAIRS - 1) as i:
                loads(i + 1)
                stores(i + 1)
            for b in range(2):
                sp.wait_ge(out_done[b], 16 * PAIRS)
            sp.wait_ge(sm["g_mm"], 4 * NB)
            sp.dma_start(w2st, a["w2"].rearrange("(f p) d -> p f d", p=P)).then_inc(sm["w2_in"], 16)
            sp.dma_start(wrs, out[0, 0:NE, :]).then_inc(sm["row_in"], 16)
            sp.wait_ge(sm["fin_ready"], 2)
            sp.dma_start(out[0, 0:NE, :], out8).then_inc(sm["fin_out"], 16)
            sp.wait_ge(sm["fin_out"], 16)

        @block.gpsimd
        def _(pool):
            pool.memset(ident[:, :], 0.0)
            pool.memset(nhalf[:, :], -0.5)
            pool.memset(minus[:, :], -1.0)
            pool.memset(sc[:, :, :], 0.0).then_inc(sm["sc_zero"], 1)
            pool.memset(sblk[:, :, :, :], 0.0)
            pool.memset(acc[:, :, :], 0.0).then_inc(sm["acc_ready"], 1)
            pool.memset(bv_b[:, :, :], 1.0)
            pool.iota(iot[:, :], pattern=[[1, NE]], base=0, channel_multiplier=0,
                      allow_small_or_imprecise_dtypes=True).then_inc(sm["s_zero"], 1)
            pool.wait_ge(sm["s_zero"], 1)
            pool.affine_select(out=ident[:, :], in_=ident[:, :], compare_op=ALU.not_equal, fill=1.0,
                               base=0, pattern=[[-1, P]], channel_multiplier=1).then_inc(sm["ident_set"], 1)

            def coefs(q, mvt, cot, n, eps, scale, what, used, mask=None):
                s_mv, s_var, s_rstd, s_coef = (sm[what + x] for x in ("_mv", "_var", "_rstd", "_coef"))
                pool.wait_ge(s_mv, q + 1)
                if used is not None:
                    need(pool, *used)
                pool.tensor_tensor(cot[:, 1, 0:n], mvt[:, 0:n, 0], minus[:, 0:n], ALU.mult)
                pool.tensor_scalar(cot[:, 0, 0:n], mvt[:, 0:n, 1], eps, scale ** -2, ALU.add, ALU.mult)\
                    .then_inc(s_var, 1)
                pool.wait_ge(s_var, q + 1)
                if mask is None:
                    pool.tensor_tensor(cot[:, 2, 0:n], cot[:, 0, 0:n], nhalf[:, 0:n], ALU.pow).then_inc(s_rstd, 1)
                else:
                    pool.tensor_tensor(cot[:, 4, 0:n], cot[:, 0, 0:n], nhalf[:, 0:n], ALU.pow)\
                        .then_inc(sm["cn_mask"], 1)
                    pool.wait_ge(sm["cn_mask"], q + 1)
                    pool.tensor_tensor(cot[:, 2, 0:n], cot[:, 4, 0:n], mask, ALU.mult).then_inc(s_rstd, 1)
                pool.wait_ge(s_rstd, q + 1)
                pool.tensor_tensor(cot[:, 3, 0:n], cot[:, 1, 0:n], cot[:, 2, 0:n], ALU.mult).then_inc(s_coef, 1)

            def largest(n, k):
                pool.wait_ge(sm["w_max"], n + 1)
                pool.partition_all_reduce(sc[:, k, 1:2], sc[:, k, 0:1], P, RMAX).then_inc(sm["w_all"], 1)

            coefs(0, mvc, coc, 8, EPS, 1.0, "ws", None)
            largest(0, 2)
            largest(1, 0)
            largest(2, 1)

            def attention(j, s):
                b, q = s % 2, 2 * j + s % 2
                if s in (0, 1):
                    coefs(q, mv, co, CH, EPS, XS, "ln1", (sm["xs_ready"], q))
                    pool.wait_ge(sm["xhi_ready"], q + 1)
                    pool.tensor_tensor(x_lo[:, b], xs[b], x_hi[:, b], ALU.subtract).then_inc(sm["xlo_ready"], 1)
                    for n in range(4):
                        c, h = n // 2, slice(TC * (n % 2), TC * (n % 2) + TC)
                        if n == 0:
                            pool.wait_ge(sm["mrow_in"], 16 * (q + 1))
                            pool.wait_ge(sm["gcol_set"], 1)
                            need(pool, sm["xpre_ready"], q)
                        else:
                            pool.wait_ge(sm["mtmp_step"], 7 * q + 2 * n)
                        pool.tensor_tensor(mtmp[:, :], mrow[:, h], gcol[:, 1, c:c + 1].broadcast_to([P, TC]), ALU.mult)\
                            .then_inc(sm["mtmp_step"], 1)
                        pool.wait_ge(sm["mtmp_step"], 7 * q + 2 * n + 1)
                        pool.tensor_tensor(xa[b][:, c, h], xa[b][:, c, h], mtmp[:, :], ALU.add)\
                            .then_inc(sm["mtmp_step" if n < 3 else "xpre_ready"], 1)
                if s in (8, 9):
                    coefs(q, mvc, coc, TT, EPS * XS * XS, 1.0, "cn", (sm["v_ready"], TT * q), m1c[:, b, :])
                if s in (10, 11):
                    coefs(q, mv2, co2, CH, EPS, XS, "ln2", (sm["xs2_ready"], q))

            for s in range(SLOTS):
                attention(0, s)
            with pool.Fori(0, PAIRS - 1) as i:
                for s in range(SLOTS):
                    attention(i + 1, s)

        @block.tensor
        def _(pe):
            def prepare():
                pe.wait_ge(sm["ident_set"], 1)
                pe.wait_ge(sm["small_in"], SMALL)
                pe.transpose(fbk[0][:, 0:P], msk, ident[:, :])
                pe.transpose(fbk[0][:, P:P + NB * CT], mskc, ident[0:NB * CT, 0:NB * CT])
                pe.transpose(fbk[0][:, 2 * P:2 * P + 6], vrow, ident[0:6, 0:6]).then_inc(sm["mask_tr"], 1)
                for d in range(FT):
                    last = pe.transpose(fbk[1][:, NE * d:NE * d + NE], wrs[:, P * d:P * d + P], ident[0:NE, 0:NE])
                last.then_inc(sm["wr_tr"], 1)
                pe.wait_ge(sm["ws_norm"], 8)
                for n in range(3):
                    for r in range(4):
                        w, o, c = (r // 2, r % 2, n) if n < 2 else (3, r % 2, r // 2)
                        last = pe.transpose(att[n][:, P * r:P * r + P], ws[:, 2 * w + o, P * c:P * c + P], ident[:, :])
                    last.then_inc(sm["ws_tr"], 1)
                pe.wait_ge(sm["ws_copy"], 3)
                for k in range(2):
                    pe.wait_ge(sm["w1_in" if k == 0 else "w3_in"], 16)
                    for n in range(2 * FT):
                        need(pe, sm["w_lo"], 16 * k + n - 3)
                        for r in range(4):
                            last = pe.transpose(att[n % 4][:, P * r:P * r + P],
                                                wst[:, 4 * (n % 2) + r, P * (n // 2):P * (n // 2) + P], ident[:, :])
                        last.then_inc(sm["w_tr"], 1)
                pe.wait_ge(sm["w_lo"], 32)

            def project(q, b, t):
                if t == 0:
                    pe.wait_ge(sm["y_in"], 16 * (q + 1))
                if t >= 2 or b == 1:
                    need(pe, sm["qk_evac"], CT * q + t - 1)
                else:
                    need(pe, sm["xt_lo_set"], 4 * q - 1 + t)
                for c in range(CH):
                    mm = pe.matmul(att[t % 2][:, :], ya[:, c, P * t:P * t + P], wqk[:, c, :],
                                   start=c == 0, stop=c == CH - 1)
                mm.then_inc(sm["qk_mm"], 1)

            def scores(q, b):
                pe.wait_ge(sm["q_ready"], CT * (q + 1))
                need(pe, *((sm["x2_ready"], 4 * q - 1) if b == 0 else (sm["sm_copy"], q)))
                for g in range(CH):
                    for t in range(CT):
                        mm = pe.matmul(att[2][:, P * g:P * g + P], qk[b][:, t, P * g:P * g + P],
                                       qk[b][:, t, S + P * g:S + P * g + P], start=t == 0, stop=t == CT - 1)
                mm.then_inc(sm["sc_mm"], 1)

            def out_times_scores(q, b):
                pe.wait_ge(sm["s_ready"], q + 1)
                need(pe, *((sm["x2_ready"], 4 * q) if b == 0 else (sm["cb_evac"], q)))
                for g in range(CH):
                    mm = pe.matmul(att[3][:, S * g:S * g + S], sblk[:, b, g, :], wo_t[:, g, :], start=True, stop=True)
                mm.then_inc(sm["t1_mm"], 1)

            def times_value(q, b):
                pe.wait_ge(sm["t1_evac"], q + 1)
                need(pe, *((sm["sm_copy"], q + 2) if b == 0 else (sm["mt_lo"], q)))
                for c in range(CH):
                    for g in range(CH):
                        mm = pe.matmul(att[2][:, S * c:S * c + S], wv_n[:, g, P * c:P * c + P], t1[:, g, :],
                                       start=g == 0, stop=g == CH - 1)
                mm.then_inc(sm["mt_mm"], 1)
                for g in range(CH):
                    mm = pe.matmul(att[3][:, 0:S], bv_b[:, g, :], t1[:, g, :], start=g == 0, stop=g == CH - 1)
                mm.then_inc(sm["cb_mm"], 1)

            def long_product(q, b, t):
                if t == 0:
                    pe.wait_ge(sm["xlo_ready"], q + 1)
                    pe.wait_ge(sm["mt_lo"], q + 1)
                if t >= 2 or b == 1:
                    need(pe, sm["u_ready"], TT * q + t - 1)
                else:
                    need(pe, sm["qk_evac"], CT * (q + 1) + 3 + t)
                bk = att[t % 2]
                for c in range(CH):
                    pe.transpose(bk[:, P * c:P * c + P], xs[b][:, c, P * t:P * t + P], ident[:, :])
                n = 0
                for c in range(CH):
                    for left, right in ((x_hi, m_hi), (x_hi, m_lo), (x_lo, m_hi)):
                        mm = pe.matmul(bk[:, S:2 * S], left[:, b, c, P * t:P * t + P], right[:, b, c, :],
                                       start=n == 0, stop=n == 5)
                        n += 1
                mm.then_inc(sm["e_mm"], 1)

            def attention_back(q, b, n):
                pe.wait_ge(sm["v_ready"], TT * q + 4 * (n % 2) + 4)
                if n >= 2 or b == 1:
                    need(pe, sm["x2_ready"], 4 * q + n - 1)
                else:
                    need(pe, sm["mt_lo" if n == 0 else "cb_evac"], q + 2)
                for r in range(4):
                    mm = pe.transpose(att[2 + n % 2][:, P * r:P * r + P],
                                      u[b][:, 4 * (n % 2) + r, P * (n // 2):P * (n // 2) + P], ident[:, :])
                mm.then_inc(sm["f_mm"], 1)

            def tokens_transposed(q, b, n):
                if n == 0:
                    pe.wait_ge(sm["xs2_ready"], q + 1)
                if n >= 2 or b == 1:
                    need(pe, sm["xt_lo_set"], 4 * q + n - 1)
                else:
                    need(pe, sm["u_ready"], TT * (q + 1) + 7 + n)
                for r in range(4):
                    t, c = 2 * n + r // 2, r % 2
                    mm = pe.transpose(att[n % 2][:, P * r:P * r + P], xs[b][:, c, P * t:P * t + P], ident[:, :])
                mm.then_inc(sm["g_mm"], 1)

            def attention(j, s, d):
                b = s % 2
                if s < 4:
                    b = s // 2
                    if s % 2 == 0 and d % 2 == 0:
                        project(2 * j + b, b, d // 2)
                    if s % 2 == 1 and d == 0:
                        scores(2 * j + b, b)
                elif s < 8:
                    b = (s - 4) // 2
                    if d == 0:
                        (out_times_scores, times_value)[s % 2](2 * j + b, b)
                elif s < 10:
                    long_product(2 * j + b, b, d)
                elif s < 12 and d % 2 == 0:
                    attention_back(2 * j + b, b, d // 2)
                elif 12 <= s < 14 and d % 2 == 0:
                    tokens_transposed(2 * j + b, b, d // 2)

            def ffn(j, g, d):
                bk = fbk[g % 2]
                if d == 0 and g > 1:
                    need(pe, sm["z_used"], GROUPS * j + g - 1)
                if g < FT:
                    if g == 0 and d == 0:
                        pe.wait_ge(sm["xt_lo_set"], 8 * (j + 1))
                    f = slice(P * g, P * g + P)
                    parts = ((w1_hi[:, d, f], xt_hi[:, d, :]), (w1_hi[:, d, f], xt_lo[:, d, :]),
                             (w1_lo[:, d, f], xt_hi[:, d, :]))
                else:
                    if g == FT:
                        pe.wait_ge(sm["h_lo"], GROUPS * j + d + 1)
                    k, f = (g - FT) // 2, slice(TOK * (g % 2), TOK * (g % 2) + TOK)
                    tok = slice(P * k, P * k + P)
                    parts = ((h1_hi[:, d, tok], w3_hi[:, d, f]), (h1_hi[:, d, tok], w3_lo[:, d, f]),
                             (h1_lo[:, d, tok], w3_hi[:, d, f]))
                for n, (left, right) in enumerate(parts):
                    mm = pe.matmul(bk[:, :], left, right, start=d == 0 and n == 0, stop=d == FT - 1 and n == 2)
                if d == FT - 1:
                    mm.then_inc(sm["z_mm"], 1)

            def router(j):
                for k in range(KT):
                    for d in range(FT):
                        for n, x in enumerate((xt_hi, xt_lo)):
                            mm = pe.matmul(rbk[:, 16 * k:16 * k + 16], x[:, d, P * k:P * k + P], wr_t[:, d, :],
                                           start=d == 0 and n == 0, stop=d == FT - 1 and n == 1)
                mm.then_inc(sm["rt_mm"], 1)

            def gated_sum(j, g):
                pe.wait_ge(sm["h_lo"], GROUPS * j + g + 1)
                if g == FT:
                    pe.wait_ge(sm["gates_ready"], j + 1)
                    pe.wait_ge(sm["acc_ready"], j + 1)
                k = (g - FT) // 2
                for m in range(4):
                    blk = 4 * (g % 2) + m
                    for n, h in enumerate((h2_hi, h2_lo)):
                        mm = pe.matmul(abk[:, 16 * blk:16 * blk + 16], h[:, g % 2, P * m:P * m + P], gts[:, k, :],
                                       start=g == FT and m == 0 and n == 0, stop=g == GROUPS - 1 and m == 3 and n == 1,
                                       skip_group_check=True)
                mm.then_inc(sm["acc_mm"], 1)

            def pair(jf, ja):
                for s in range(SLOTS):
                    for d in range(FT):
                        if ja is not None:
                            attention(ja, s, d)
                        if jf is not None:
                            ffn(jf, s, d)
                    if jf is not None:
                        if s == 1:
                            router(jf)
                        if s > FT:
                            gated_sum(jf, s - 1)
                if jf is not None:
                    gated_sum(jf, GROUPS - 1)

            prepare()
            pair(None, 0)
            with pe.Fori(0, PAIRS - 1) as i:
                pair(i, i + 1)
            pair(PAIRS - 1, None)

            pe.wait_ge(sm["w2_in"], 16)
            for n in range(2 * FT):
                k, h = n // 2, n % 2
                need(pe, sm["w2_copy"], n - 3)
                for r in range(4):
                    mm = pe.transpose(att[n % 4][:, P * r:P * r + P], w2st[:, 4 * h + r, P * k:P * k + P], ident[:, :])
                mm.then_inc(sm["w2_tr"], 1)
            pe.wait_ge(sm["acs_set"], 1)
            pe.wait_ge(sm["w2_copy"], 2 * FT)
            for h in range(2):
                for k in range(FT):
                    mm = pe.matmul(fbk[h][0:NE, :], acs[:, k, :], w2t[k // 4][:, k % 4, 512 * h:512 * h + 512],
                                   start=k == 0, stop=k == FT - 1)
                mm.then_inc(sm["fin_mm"], 1)

        @block.scalar
        def _(act):
            smalls = [(wn[:, 2 * n:2 * n + 2, :], a[w].rearrange("(c p) n -> p c n", p=P))
                      for n, w in enumerate(("wq", "wk", "wv", "wo"))]
            smalls += [(wrs, a["wr"]), (msk, a["mask"].rearrange("q o (t p) -> (q o t) p", p=P)),
                       (mskc, a["mask_cond"].rearrange("q o (t p) -> (q o t) p", p=P)),
                       (qkb_b[:, 0:S], a["bq"].partition_broadcast(P)), (qkb_b[:, S:2 * S], a["bk"].partition_broadcast(P)),
                       (bo_b[:, :], a["bo"].partition_broadcast(P)),
                       (vrow[0:2, :], a["bv"].rearrange("(c p) -> c p", p=P)),
                       (vrow[2:4, :], a["gamma"].rearrange("(c p) -> c p", p=P)),
                       (vrow[4:6, :], a["beta"].rearrange("(c p) -> c p", p=P)),
                       (graw[:, 0:1], a["g_xattn"].partition_broadcast(P)),
                       (graw[:, 1:2], a["g_ffn"].partition_broadcast(P))]
            assert SMALL == 16 * len(smalls)
            for dst, src in smalls:
                act.dma_start(dst, src).then_inc(sm["small_in"], 16)
            act.wait_ge(sm["small_in"], SMALL)
            act.activation(tg[:, :], graw, ACT.Tanh).then_inc(sm["tg_set"], 1)
            act.wait_ge(sm["ws_coef"], 1)
            for n in range(8):
                dst = wv_n[:, n - 4, :] if n in (4, 5) else ws[:, n, :]
                act.activation(dst, wn[:, n, :], ACT.Identity, bias=coc[:, 3, n:n + 1], scale=coc[:, 2, n:n + 1])\
                    .then_inc(sm["ws_norm"], 1)
            for n in range(3):
                act.wait_ge(sm["ws_tr"], n + 1)
                dst = wqk[:, n, :] if n < 2 else wo_t[:, :, :]
                src = att[n][:, :] if n < 2 else att[n][:, :].rearrange("p (c n) -> p c n", c=CH)
                act.activation(dst, src, ACT.Copy).then_inc(sm["ws_copy"], 1)
            act.wait_ge(sm["w_scale"], 1)
            act.wait_ge(sm["wr_tr"], 1)
            act.activation(wr_t[:, :, 0:NE], fbk[1][:, 0:FT * NE].rearrange("p (d n) -> p d n", d=FT), ACT.Copy,
                           scale=sc[:, 2, 2:3]).then_inc(sm["wr_hi"], 1)
            for k, dst in enumerate((w1_hi, w3_hi)):
                act.wait_ge(sm["w_scale"], k + 2)
                for n in range(2 * FT):
                    act.wait_ge(sm["w_tr"], 16 * k + n + 1)
                    act.activation(dst[:, n // 2, 512 * (n % 2):512 * (n % 2) + 512], att[n % 4][:, :], ACT.Copy,
                                   scale=sc[:, k, 2:3]).then_inc(sm["w_hi"], 1)
                if k == 0:
                    act.wait_ge(sm["w_lo"], 16)
                    act.dma_start(wst, a["w3"].rearrange("(f p) d -> p f d", p=P)).then_inc(sm["w3_in"], 16)

            def normed(q, b, c_, s_coef, s_done):
                act.wait_ge(s_coef, q + 1)
                for c in range(CH):
                    ins = act.activation(xs[b][:, c, :], xa[b][:, c, :], ACT.Identity,
                                         bias=c_[:, 3, c:c + 1], scale=c_[:, 2, c:c + 1])
                ins.then_inc(s_done, 1)

            def attention(j, s):
                b, q = s % 2, 2 * j + s % 2
                if s in (0, 1):
                    normed(q, b, co, sm["ln1_coef"], sm["xs_ready"])
                if s < 4:
                    b = s // 2
                    q = 2 * j + b
                    if s % 2 == 0:
                        for t in range(CT):
                            act.wait_ge(sm["qk_evac"], CT * q + t + 1)
                            act.activation(qk[b][:, t, 0:S], qk[b][:, t, 0:S], ACT.Copy, scale=mcc[:, b, t:t + 1])\
                                .then_inc(sm["q_ready"], 1)
                    else:
                        act.wait_ge(sm["sm_sub"], q + 1)
                        act.activation(dg[:, :, :], dg[:, :, :], ACT.Exp, scale=SCORE).then_inc(sm["sm_exp"], 1)
                elif s < 8:
                    b = (s - 4) // 2
                    q = 2 * j + b
                    if s % 2 == 0:
                        act.wait_ge(sm["t1_mm"], q + 1)
                        act.activation(t1[:, :, :], att[3][:, :].rearrange("p (c n) -> p c n", c=CH), ACT.Copy)\
                            .then_inc(sm["t1_evac"], 1)
                    else:
                        act.wait_ge(sm["mt_mm"], q + 1)
                        act.activation(m_hi[:, b], att[2][:, :].rearrange("p (c n) -> p c n", c=CH), ACT.Copy, scale=MS)\
                            .then_inc(sm["mt_hi"], 1)
                        act.wait_ge(sm["cb_mm"], q + 1)
                        act.activation(cb[:, b, :], att[3][:, 0:S], ACT.Copy, scale=XS).then_inc(sm["cb_evac"], 1)
                if s in (9, 10):
                    b, q = s - 9, 2 * j + s - 9
                    act.wait_ge(sm["cn_coef"], q + 1)
                    for t in range(TT):
                        act.activation(u[b][:, t, :], u[b][:, t, :], ACT.Identity, bias=coc[:, 3, t:t + 1],
                                       scale=coc[:, 2, t:t + 1]).then_inc(sm["v_ready"], 1)
                if s in (11, 12):
                    normed(2 * j + s - 11, s - 11, co2, sm["ln2_coef"], sm["xs2_ready"])
                if s in (12, 13):
                    b, q = s - 12, 2 * j + s - 12
                    for n in range(4):
                        act.wait_ge(sm["g_mm"], 4 * q + n + 1)
                        act.activation(xt_hi[:, 2 * n:2 * n + 2, S * b:S * b + S],
                                       att[n % 2][:, :].rearrange("p (t n) -> p t n", t=2), ACT.Copy)\
                            .then_inc(sm["xt_hi_set"], 1)

            def ffn(j, g):
                act.wait_ge(sm["z_mm"], GROUPS * j + g + 1)
                act.activation(act_t[:, g % 2, :], fbk[g % 2][:, :], ACT.Tanh,
                               scale=fs[:, 0:1] if g < FT else fs[:, 1:2]).then_inc(sm["th_ready"], 1)
                if g >= FT + 2:
                    act.wait_ge(sm["acc_mm"], 8 * j + g - FT - 1)
                act.wait_ge(sm["z_used"], GROUPS * j + g + 1)
                act.activation(h1_hi[:, g, :] if g < FT else h2_hi[:, g % 2, :], act_t[:, g % 2, :], ACT.Copy,
                               scale=H1S if g < FT else H2S).then_inc(sm["h_hi"], 1)

            def gates(j):
                act.wait_ge(sm["rt_gap"], j + 1)
                act.activation(gd[:, 1, :], gd[:, 0, :], ACT.Exp, scale=fs[:, 2:3]).then_inc(sm["rt_exp"], 1)

            def pair(jf, ja):
                for s in range(SLOTS):
                    if ja is not None:
                        attention(ja, s)
                    if jf is not None:
                        ffn(jf, s)
                        if s == 2:
                            gates(jf)

            pair(None, 0)
            act.wait_ge(sm["fs_set"], 1)
            with act.Fori(0, PAIRS - 1) as i:
                pair(i, i + 1)
            pair(PAIRS - 1, None)
            for n in range(2 * FT):
                act.wait_ge(sm["w2_tr"], n + 1)
                k, h = n // 2, n % 2
                act.activation(w2t[k // 4][:, k % 4, 512 * h:512 * h + 512], att[n % 4][:, :], ACT.Copy)\
                    .then_inc(sm["w2_copy"], 1)

        @block.vector
        def _(dve):
            def carry():
                dve.memset(spare[:, :], 0.0)

            def prepare():
                dve.wait_ge(sm["small_in"], SMALL)
                for n in range(8):
                    ins = dve.bn_stats(bst[:, n, :], wn[:, n, :])
                ins.then_inc(sm["ws_stat"], 1)
                dve.wait_ge(sm["ws_stat"], 1)
                for n in range(8):
                    ins = dve.bn_aggr(mvc[:, n, :], bst[:, n, :])
                ins.then_inc(sm["ws_mv"], 1)
                dve.wait_ge(sm["mask_tr"], 1)
                dve.tensor_copy(vcol, fbk[0][:, 2 * P:2 * P + 6])
                dve.tensor_copy(mtab[:, :, 0:16], fbk[0][:, 0:P].rearrange("p (j n) -> p j n", j=PAIRS))
                dve.tensor_copy(mtab[:, :, 48:56], fbk[0][:, P:P + 64].rearrange("p (j n) -> p j n", j=PAIRS))\
                    .then_inc(sm["mask_copy"], 1)
                dve.wait_ge(sm["mask_copy"], 1)
                dve.tensor_tensor(mtab[:, :, 16:32], mtab[:, :, 0:16], mtab[:, :, 0:16], ALU.mult)
                dve.tensor_tensor(mtab[:, :, 48:56], mtab[:, :, 48:56], mtab[:, :, 48:56], ALU.mult)\
                    .then_inc(sm["mask_sq"], 1)
                dve.wait_ge(sm["mask_sq"], 1)
                dve.tensor_scalar(mtab[:, :, 32:48], mtab[:, :, 16:32], 1.0 / MS, None, ALU.mult)\
                    .then_inc(sm["mask_sq"], 1)
                dve.wait_ge(sm["mask_sq"], 2)
                dve.wait_ge(sm["tg_set"], 1)
                dve.tensor_scalar(gcol[:, :, :], vcol[:, 2:6].rearrange("p (a c) -> p a c", a=2), tg[:, 0:1], None, ALU.mult).then_inc(sm["gcol_set"], 1)
                dve.tensor_scalar(bo_b[:, :], bo_b[:, :], XS, None, ALU.mult)
                dve.wait_ge(sm["s_zero"], 1)
                for g in range(CH):
                    ins = dve.tensor_scalar(bv_b[:, g, :], bv_b[:, g, :], vcol[:, g:g + 1], None, ALU.mult)
                ins.then_inc(sm["bias_set"], 1)
                dve.wait_ge(sm["bias_set"], 1)
                dve.wait_ge(sm["sc_zero"], 1)

                def scale_of(n, k, src, parts):
                    dve.tensor_reduce(sc[0:parts, k, 0:1], src, AX.XY if parts == P else AX.X, ALU.max,
                                      apply_absolute_value=True).then_inc(sm["w_max"], 1)
                    dve.wait_ge(sm["w_all"], n + 1)
                    dve.tensor_scalar(sc[:, k, 0:1], sc[:, k, 1:2], 1e-30, None, ALU.max).then_inc(sm["w_clamp"], 1)
                    dve.wait_ge(sm["w_clamp"], n + 1)
                    si = sc[:, k, :].bitcast(I32)
                    dve.tensor_scalar(si[:, 0:1], si[:, 0:1], 0x7F800000, None, ALU.bitwise_and)\
                        .then_inc(sm["w_bits"], 1)
                    dve.wait_ge(sm["w_bits"], n + 1)
                    dve.tensor_scalar(si[:, 2:3], si[:, 0:1], -1.0, float(268 << 23), ALU.mult, ALU.add)
                    dve.tensor_scalar(si[:, 3:4], si[:, 0:1], -float(14 << 23), None, ALU.add)\
                        .then_inc(sm["w_scale"], 1)
                    dve.wait_ge(sm["w_scale"], n + 1)

                scale_of(0, 2, wrs, NE)
                dve.wait_ge(sm["wr_hi"], 1)
                dve.scalar_tensor_tensor(out=wr_t[:, :, NE:2 * NE], in0=fbk[1][:, 0:FT * NE].rearrange("p (d n) -> p d n", d=FT),
                                         scalar=sc[:, 2, 2:3], in1=wr_t[:, :, 0:NE], op0=ALU.mult, op1=ALU.subtract)\
                    .then_inc(sm["wr_lo"], 1)
                for k, (hi, lo) in enumerate(((w1_hi, w1_lo), (w3_hi, w3_lo))):
                    dve.wait_ge(sm["w1_in" if k == 0 else "w3_in"], 16)
                    scale_of(k + 1, k, wst, P)
                    for n in range(2 * FT):
                        dve.wait_ge(sm["w_hi"], 16 * k + n + 1)
                        at = slice(512 * (n % 2), 512 * (n % 2) + 512)
                        dve.scalar_tensor_tensor(out=lo[:, n // 2, at], in0=att[n % 4][:, :], scalar=sc[:, k, 2:3],
                                                 in1=hi[:, n // 2, at], op0=ALU.mult, op1=ALU.subtract)\
                            .then_inc(sm["w_lo"], 1)
                dve.tensor_scalar(fs[:, 0:1], sc[:, 0, 3:4], 2.0 ** -11, None, ALU.mult)
                dve.tensor_scalar(fs[:, 2:3], sc[:, 2, 3:4], 1.0 / XS, None, ALU.mult)
                dve.tensor_scalar(fs[:, 1:2], sc[:, 0, 3:4], sc[:, 1, 3:4], 2.0 ** 9, ALU.mult, ALU.mult)\
                    .then_inc(sm["fs_part"], 1)
                dve.wait_ge(sm["fs_part"], 1)
                dve.tensor_scalar(fs[:, 3:4], fs[:, 1:2], tg[:, 1:2], 2.0 ** 26, ALU.mult, ALU.mult)\
                    .then_inc(sm["fs_set"], 1)

            def ln1(j, b):
                q = 2 * j + b
                dve.wait_ge(x_in[b], 16 * (j + 1))
                for n in range(4):
                    ins = dve.bn_stats(bst[:, n, :], xa[b][:, n // 2, TC * (n % 2):TC * (n % 2) + TC])
                ins.then_inc(sm["ln1_stat"], 1)
                dve.wait_ge(sm["ln1_stat"], q + 1)
                need(dve, sm["ln1_coef"], q)
                carry()
                for c in range(CH):
                    ins = dve.bn_aggr(mv[:, c, :], bst[:, 2 * c:2 * c + 2, :])
                ins.then_inc(sm["ln1_mv"], 1)

            def x_high(q, b):
                dve.wait_ge(sm["xs_ready"], q + 1)
                dve.tensor_copy(x_hi[:, b], xs[b]).then_inc(sm["xhi_ready"], 1)

            def softmax(q, b):
                dve.wait_ge(sm["sc_mm"], q + 1)
                for h in range(4):
                    r = slice(HD * h, HD * h + HD)
                    ins = dve.tensor_copy(dg[r, :, :], att[2][r, 0:2 * P].rearrange("p (g n) -> p g n", g=CH)[:, :, r])
                ins.then_inc(sm["sm_copy"], 1)
                dve.wait_ge(sm["sm_copy"], q + 1)
                dve.tensor_reduce(dr[:, 0, :], dg[:, :, :], AX.X, ALU.max).then_inc(sm["sm_max"], 1)
                dve.wait_ge(sm["sm_max"], q + 1)
                dve.tensor_tensor(dg[:, :, :], dg[:, :, :], dr[:, 0, :].unsqueeze(2).broadcast_to([P, CH, HD]),
                                  ALU.subtract).then_inc(sm["sm_sub"], 1)
                dve.wait_ge(sm["sm_exp"], q + 1)
                dve.tensor_reduce(dr[:, 1, :], dg[:, :, :], AX.X, ALU.add).then_inc(sm["sm_sum"], 1)
                dve.wait_ge(sm["sm_sum"], q + 1)
                dve.reciprocal(dr[:, 2, :], dr[:, 1, :]).then_inc(sm["sm_rec"], 1)
                dve.wait_ge(sm["sm_rec"], q + 1)
                for h in range(4):
                    r = slice(HD * h, HD * h + HD)
                    ins = dve.tensor_tensor(sblk[r, b, :, r], dg[r, :, :],
                                            dr[r, 2, :].unsqueeze(2).broadcast_to([HD, CH, HD]), ALU.mult)
                ins.then_inc(sm["s_ready"], 1)

            def attention_out(q, b):
                dve.wait_ge(sm["cb_evac"], q + 1)

                def stats(t):
                    dve.wait_ge(sm["u_ready"], TT * q + t + 1)
                    dve.bn_stats(bst2[:, t, :], u[b][:, t, :]).then_inc(sm["u_stat"], 1)

                for t in range(TT):
                    bk = att[t % 2]
                    dve.wait_ge(sm["e_mm"], TT * q + t + 1)
                    dve.scalar_tensor_tensor(out=ea[:, :], in0=bo_b[:, :], scalar=m1c[:, b, t:t + 1], in1=bk[:, 0:S],
                                             op0=ALU.mult, op1=ALU.add).then_inc(sm["e_bo"], 1)
                    if t > 0:
                        stats(t - 1)
                    dve.wait_ge(sm["e_bo"], TT * q + t + 1)
                    dve.scalar_tensor_tensor(out=eb[:, :], in0=cb[:, b, :], scalar=m2c[:, b, t:t + 1], in1=ea[:, :],
                                             op0=ALU.mult, op1=ALU.add).then_inc(sm["e_cb"], 1)
                    dve.wait_ge(sm["e_cb"], TT * q + t + 1)
                    dve.scalar_tensor_tensor(out=u[b][:, t, :], in0=bk[:, S:2 * S], scalar=m2s[:, b, t:t + 1],
                                             in1=eb[:, :], op0=ALU.mult, op1=ALU.add).then_inc(sm["u_ready"], 1)
                stats(TT - 1)
                dve.wait_ge(sm["u_stat"], TT * (q + 1))
                need(dve, sm["cn_coef"], q)
                carry()
                for t in range(TT):
                    ins = dve.bn_aggr(mvc[:, t, :], bst2[:, t, :])
                ins.then_inc(sm["cn_mv"], 1)

            def residual(q, b):
                dve.wait_ge(sm["xpre_ready"], q + 1)

                def stats(n):
                    dve.wait_ge(sm["x2_ready"], 4 * q + n + 1)
                    dve.bn_stats(bst[:, n, :], xa[b][:, n // 2, TC * (n % 2):TC * (n % 2) + TC])\
                        .then_inc(sm["ln2_stat"], 1)

                for n in range(4):
                    c, h = n // 2, slice(TC * (n % 2), TC * (n % 2) + TC)
                    dve.wait_ge(sm["f_mm"], 4 * q + n + 1)
                    dve.scalar_tensor_tensor(out=xa[b][:, c, h], in0=att[2 + n % 2][:, :], scalar=gcol[:, 0, c:c + 1],
                                             in1=xa[b][:, c, h], op0=ALU.mult, op1=ALU.add).then_inc(sm["x2_ready"], 1)
                    if n > 0:
                        stats(n - 1)
                stats(3)
                dve.wait_ge(sm["ln2_stat"], 4 * (q + 1))
                need(dve, sm["ln2_coef"], q)
                carry()
                for c in range(CH):
                    ins = dve.bn_aggr(mv2[:, c, :], bst[:, 2 * c:2 * c + 2, :])
                ins.then_inc(sm["ln2_mv"], 1)

            def attention(j, s):
                if s == 0:
                    need(dve, sm["cn_coef"], 2 * j)
                    need(dve, sm["q_ready"], 2 * CT * j)
                    dve.tensor_copy(mcur[:, :], mtab[:, j, :]).then_inc(sm["mcur_set"], 1)
                    dve.wait_ge(sm["mcur_set"], j + 1)
                if s in (0, 1):
                    ln1(j, s)
                if s < 4:
                    b = s // 2
                    q = 2 * j + b
                    if s % 2 == 0:
                        for t in range(CT):
                            dve.wait_ge(sm["qk_mm"], CT * q + t + 1)
                            dve.tensor_tensor(qk[b][:, t, :], att[t % 2][:, :], qkb_b[:, :], ALU.add)\
                                .then_inc(sm["qk_evac"], 1)
                    else:
                        softmax(q, b)
                if s in (0, 1):
                    x_high(2 * j + s, s)
                if s in (5, 7):
                    b = (s - 5) // 2
                    q = 2 * j + b
                    dve.wait_ge(sm["mt_hi"], q + 1)
                    dve.scalar_tensor_tensor(out=m_lo[:, b], in0=att[2][:, :].rearrange("p (c n) -> p c n", c=CH), scalar=MS,
                                             in1=m_hi[:, b], op0=ALU.mult, op1=ALU.subtract).then_inc(sm["mt_lo"], 1)
                if s in (8, 9):
                    attention_out(2 * j + s - 8, s - 8)
                if s in (10, 11):
                    residual(2 * j + s - 10, s - 10)
                if s in (12, 13):
                    b, q = s - 12, 2 * j + s - 12
                    for n in range(4):
                        dve.wait_ge(sm["xt_hi_set"], 4 * q + n + 1)
                        dve.tensor_tensor(xt_lo[:, 2 * n:2 * n + 2, S * b:S * b + S],
                                          att[n % 2][:, :].rearrange("p (t n) -> p t n", t=2),
                                          xt_hi[:, 2 * n:2 * n + 2, S * b:S * b + S], ALU.subtract)\
                            .then_inc(sm["xt_lo_set"], 1)

            def ffn(j, g):
                buf = act_t[:, g % 2, :]
                dve.wait_ge(sm["th_ready"], GROUPS * j + g + 1)
                dve.scalar_tensor_tensor(out=buf, in0=buf, scalar=1.0, in1=fbk[g % 2][:, :], op0=ALU.add, op1=ALU.mult)\
                    .then_inc(sm["z_used"], 1)
                dve.wait_ge(sm["h_hi"], GROUPS * j + g + 1)
                hi = h1_hi[:, g, :] if g < FT else h2_hi[:, g % 2, :]
                lo = h1_lo[:, g, :] if g < FT else h2_lo[:, g % 2, :]
                dve.scalar_tensor_tensor(out=lo, in0=buf, scalar=H1S if g < FT else H2S, in1=hi,
                                         op0=ALU.mult, op1=ALU.subtract).then_inc(sm["h_lo"], 1)

            def top_two(j):
                dve.wait_ge(sm["rt_mm"], j + 1)
                dve.tensor_copy(lg[:, :, :], rbk[:, 0:KT * 16].rearrange("p (k n) -> p k n", k=KT))\
                    .then_inc(sm["rt_copy"], 1)
                dve.wait_ge(sm["rt_copy"], j + 1)
                dve.tensor_tensor(lgs[:, :, :], lg[:, :, 0:NE], lg[:, :, NE:2 * NE], ALU.add).then_inc(sm["rt_sum"], 1)
                dve.wait_ge(sm["rt_sum"], j + 1)
                carry()
                for k in range(KT):
                    ins = dve.max(top[:, k, :], lgs[:, k, :])
                ins.then_inc(sm["rt_max"], 1)
                dve.wait_ge(sm["rt_max"], j + 1)
                dve.tensor_tensor(gd[:, 0, :], top[:, :, 1], top[:, :, 0], ALU.subtract).then_inc(sm["rt_gap"], 1)
                for k in range(KT):
                    ins = dve.max_index(topi[:, k, :], top[:, k, :], lgs[:, k, :])
                ins.then_inc(sm["rt_idx"], 1)
                dve.wait_ge(sm["rt_idx"], j + 1)
                dve.tensor_copy(topf[:, :, :], topi[:, :, 0:2]).then_inc(sm["rt_idx2"], 1)

            def gates(j):
                dve.wait_ge(sm["rt_exp"], j + 1)
                dve.tensor_scalar(gd[:, 0, :], gd[:, 1, :], 1.0, None, ALU.add).then_inc(sm["rt_den"], 1)
                dve.wait_ge(sm["rt_den"], j + 1)
                dve.reciprocal(gd[:, 2, :], gd[:, 0, :]).then_inc(sm["rt_g1"], 1)
                dve.wait_ge(sm["rt_idx2"], j + 1)
                for n, e in enumerate((e1t, e2t)):
                    ins = dve.tensor_tensor(e[:, :, :], iot[:, :].unsqueeze(1).broadcast_to([P, KT, NE]),
                                            topf[:, :, n].unsqueeze(2).broadcast_to([P, KT, NE]), ALU.is_equal)
                ins.then_inc(sm["rt_eq"], 1)
                dve.wait_ge(sm["rt_g1"], j + 1)
                dve.tensor_tensor(gd[:, 3, :], gd[:, 1, :], gd[:, 2, :], ALU.mult).then_inc(sm["rt_g2"], 1)
                dve.wait_ge(sm["rt_eq"], j + 1)
                dve.wait_ge(sm["rt_g2"], j + 1)
                for n, e in enumerate((e1t, e2t)):
                    ins = dve.tensor_tensor(e[:, :, :], e[:, :, :], gd[:, 2 + n, :].unsqueeze(2).broadcast_to([P, KT, NE]),
                                            ALU.mult)
                ins.then_inc(sm["rt_sel"], 1)
                dve.wait_ge(sm["rt_sel"], j + 1)
                dve.tensor_tensor(e1t[:, :, :], e1t[:, :, :], e2t[:, :, :], ALU.add).then_inc(sm["rt_gate"], 1)
                dve.wait_ge(sm["rt_gate"], j + 1)
                dve.tensor_copy(gts[:, :, 0:NE], e1t[:, :, :]).then_inc(sm["gates_hi"], 1)
                dve.wait_ge(sm["gates_hi"], j + 1)
                dve.tensor_tensor(gts[:, :, NE:2 * NE], e1t[:, :, :], gts[:, :, 0:NE], ALU.subtract)\
                    .then_inc(sm["gates_ready"], 1)

            def pair(jf, ja):
                for s in range(SLOTS):
                    if ja is not None:
                        attention(ja, s)
                    if jf is not None:
                        if s == 3:
                            gates(jf)
                        ffn(jf, s)
                        if s == 2:
                            top_two(jf)
                if jf is not None:
                    dve.wait_ge(sm["acc_mm"], 8 * (jf + 1))
                    dve.wait_ge(sm["acc_ready"], jf + 1)
                    dve.tensor_tensor(acc[:, :, :], acc[:, :, :], abk[:, 0:P].rearrange("p (k n) -> p k n", k=FT),
                                      ALU.add).then_inc(sm["acc_ready"], 1)

            prepare()
            pair(None, 0)
            with dve.Fori(0, PAIRS - 1) as i:
                pair(i, i + 1)
            pair(PAIRS - 1, None)

            dve.wait_ge(sm["acc_ready"], PAIRS + 1)
            dve.tensor_tensor(acs[:, :, :], acc[:, :, 0:NE], acc[:, :, NE:2 * NE], ALU.add).then_inc(sm["acs_set"], 1)
            dve.wait_ge(sm["row_in"], 16)
            for h in range(2):
                dve.wait_ge(sm["fin_mm"], h + 1)
                at = slice(512 * h, 512 * h + 512)
                dve.scalar_tensor_tensor(out=out8[:, at], in0=fbk[h][0:NE, :], scalar=fs[0:NE, 3:4], in1=wrs[:, at],
                                         op0=ALU.mult, op1=ALU.add).then_inc(sm["fin_ready"], 1)


_INS = {"x": "x", "ctx": "ctx_1024", "mask": "mask_Bx1x2048_ff1", "mask_cond": "mask_Bx1x1024_ff1",
        "g_xattn": "g_xattn", "g_ffn": "g_ffn",
        "wq": "L0_xattn_wq", "bq": "L0_xattn_bq", "wk": "L0_xattn_wk", "bk": "L0_xattn_bk",
        "wv": "L0_xattn_wv", "bv": "L0_xattn_bv", "wo": "L0_xattn_wo", "bo": "L0_xattn_bo",
        "gamma": "L0_xattn_gamma", "beta": "L0_xattn_beta",
        "w1": "L0_ffn_w1", "w3": "L0_ffn_w3", "w2": "L0_ffn_w2", "wr": "L0_ffn_wr"}


def kernel(**inputs):
    import numpy as _np
    import concourse.bacc as _bacc
    from concourse import mybir as _mybir
    from concourse.bass_utils import run_bass_kernel_spmd as _run

    nc = _bacc.Bacc("TRN2", target_bir_lowering=False, num_devices=1)
    arrays, aps = {}, {}
    for short, name in _INS.items():
        v = _np.ascontiguousarray(inputs[name])
        arrays[f"in_{short}_dram"] = v
        aps[short] = nc.dram_tensor(f"in_{short}_dram", v.shape, _mybir.dt.from_np(v.dtype), kind="ExternalInput").ap()
    out = nc.dram_tensor("out_0_dram", (NB, S, T), _mybir.dt.from_np(_np.dtype("float32")), kind="ExternalOutput").ap()
    build(nc, aps, out)
    r = _run(nc, [arrays], core_ids=[0])
    return r.results[0]["out_0_dram"]
```

```python
from contextlib import ExitStack

import concourse.bass as bass
from concourse import mybir

ALU = mybir.AluOpType
ACT = mybir.ActivationFunctionType
AX = mybir.AxisListType
F32 = mybir.dt.float32
F16 = mybir.dt.float16
I32 = mybir.dt.int32
U32 = mybir.dt.uint32
RMAX = bass.bass_isa.ReduceOp.max

P = 128
NB = 16
S = 256
T = 1024
TC = 512
HD = 32
NE = 8
CH = S // P
TT = T // P
CT = TC // P
PAIRS = NB // 2
TOK = 2 * S
FT = T // P
KT = TOK // P
GROUPS = FT + 2 * KT
STAGES = 14
EPS = 1e-5
SCORE = 1.0 / float(S // 8 ** 0.5)
XS = 1024.0
MS = 8.0
SMALL = 16 * 15
W_MAX = (2, 6)
W_TR = range(3, 11)
H1S = 2.0 ** -21
H2S = 2.0 ** -26


def build(nc, a, out):
    ctx = ExitStack()

    def sb(name, shape, dt=F32):
        return ctx.enter_context(nc.sbuf_tensor(name, shape, dt))

    def sem(name):
        return ctx.enter_context(nc.semaphore(name))

    def need(eng, s, count):
        if isinstance(count, int) and count <= 0:
            return
        eng.wait_ge(s, count)

    with ctx:
        w1b = sb("w1b", [P, 2, FT, T], F16)
        w1_hi, w1_lo = w1b[:, 0], w1b[:, 1]
        w3_hi = sb("w3_hi", [P, FT, T], F16)
        w3_lo = sb("w3_lo", [P, FT, T], F16)
        stage = sb("stage", [P, 4 * 2048], F32)
        half = stage[:, :].bitcast(F16)
        xt_hi = half[:, 0:4096].rearrange("p (t n) -> p t n", t=TT)
        xt_lo = half[:, 4096:8192].rearrange("p (t n) -> p t n", t=TT)
        h1_hi = half[:, 8192:12288].rearrange("p (t n) -> p t n", t=FT)
        h1_lo = half[:, 12288:16384].rearrange("p (t n) -> p t n", t=FT)
        w1n = stage[:, :].rearrange("p (t n) -> p t n", t=FT)
        wide = w1b[:, :, :, :].rearrange("p a t n -> p (a t n)").bitcast(F32).rearrange("p (t n) -> p t n", t=FT)
        w3n, w2t = wide, wide
        xbuf = sb("xbuf", [P, 2, 2, CH, T], F32)
        xa = [xbuf[:, 0, b] for b in range(2)]
        xs = [xbuf[:, 1, b] for b in range(2)]
        w2st = xbuf[:, :, :, :, :].rearrange("p a b c t -> p (a b c) t")
        x_hi = sb("x_hi", [P, 2, CH, T], F16)
        x_lo = sb("x_lo", [P, 2, CH, T], F16)
        ya = sb("ya", [P, CH, TC])
        ub = sb("ub", [P, 2, 2048])
        qk = [ub[:, b, :].rearrange("p (t n) -> p t n", t=CT) for b in range(2)]
        u = [ub[:, b, :].rearrange("p (t n) -> p t n", t=TT) for b in range(2)]
        mrow = sb("mrow", [P, T])
        mtmp = sb("mtmp", [P, TC])
        act_t = sb("act_t", [P, 2, TOK])
        h2_hi = sb("h2_hi", [P, 2, TOK], F16)
        h2_lo = sb("h2_lo", [P, 2, TOK], F16)
        sblk = sb("sblk", [P, 2, CH, P])
        t1 = sb("t1", [P, CH, S])
        m_hi = sb("m_hi", [P, 2, CH, S], F16)
        m_lo = sb("m_lo", [P, 2, CH, S], F16)
        cb = sb("cb", [P, 2, S])
        bo_b = sb("bo_b", [P, S])
        qkb_b = sb("qkb_b", [P, 2 * S])
        wqk = sb("wqk", [P, CH, 2 * S])
        wo_t = sb("wo_t", [P, CH, S])
        wv_n = sb("wv_n", [P, CH, S])
        bv_b = sb("bv_b", [P, CH, P])
        wr_t = sb("wr_t", [P, FT, 2 * NE], F16)
        acc = sb("acc", [P, FT, 2 * NE])
        ident = sb("ident", [P, P])
        mtab = sb("mtab", [P, PAIRS, 56])
        mcur = sb("mcur", [P, 56])
        m1c = mcur[:, 0:16].rearrange("p (b t) -> p b t", b=2)
        m2c = mcur[:, 16:32].rearrange("p (b t) -> p b t", b=2)
        m2s = mcur[:, 32:48].rearrange("p (b t) -> p b t", b=2)
        mcc = mcur[:, 48:56].rearrange("p (b t) -> p b t", b=2)
        minus = sb("minus", [P, 8])
        nhalf = sb("nhalf", [P, 8])
        bst = sb("bst", [P, 8, 6])
        bst2 = sb("bst2", [P, 8, 6])
        mv = sb("mv", [P, 2, 2])
        mv2 = sb("mv2", [P, 2, 2])
        mvc = sb("mvc", [P, 8, 2])
        co = sb("co", [P, 4, 2])
        co2 = sb("co2", [P, 4, 2])
        coc = sb("coc", [P, 5, 8])
        dg = sb("dg", [P, CH, HD])
        dr = sb("dr", [P, 3, CH])
        gcol = sb("gcol", [P, 2, CH])
        tg = sb("tg", [P, 2])
        sc = sb("sc", [P, 3, 4])
        fs = sb("fs", [P, 4])
        lg = sb("lg", [P, KT, 2 * NE])
        lgs = sb("lgs", [P, KT, NE])
        top = sb("top", [P, KT, 8])
        topi = sb("topi", [P, KT, 8], U32)
        topf = sb("topf", [P, KT, 2])
        spare = sb("spare", [P, 1])
        gd = sb("gd", [P, 4, KT])
        iot = sb("iot", [P, NE])
        e1t = sb("e1t", [P, KT, NE])
        e2t = sb("e2t", [P, KT, NE])
        gts = sb("gts", [P, KT, 2 * NE], F16)
        acs = sb("acs", [P, FT, NE])
        wrs = x_hi[0:NE, 0].rearrange("p c t -> p (c t)").bitcast(F32)
        out8 = x_lo[0:NE, 0].rearrange("p c t -> p (c t)").bitcast(F32)

        bank = [ctx.enter_context(nc.psum_tensor(f"bank{n}", [P, 512], F32)) for n in range(8)]
        att = bank[0:4]
        fbk = bank[4:6]
        rbk, abk = bank[6], bank[7]
        wbk = bank[4:8]

        x_in = [sem(f"x_in{b}") for b in range(2)]
        out_done = [sem(f"out_done{b}") for b in range(2)]
        names = """y_in mrow_in w1_in w3_in small_in
            ident_set s_zero sc_zero w_max w_all w_clamp w_bits w_scale w_tr w_hi w_lo wr_tr wr_hi wr_lo
            ws_stat ws_mv ws_var ws_rstd ws_coef ws_norm ws_tr ws_copy
            mask_tr mask_copy mask_sq tg_set gcol_set bias_set fs_part fs_set
            mcur_set ln1_stat ln1_mv ln1_var ln1_rstd ln1_coef xs_ready xhi_ready xlo_ready mtmp_step xpre_ready
            qk_mm qk_evac q_ready sc_mm sm_copy sm_max sm_sub sm_exp sm_sum sm_rec s_ready
            t1_mm t1_evac mt_mm mt_hi mt_lo cb_mm cb_evac
            ub_part ub_ready e_mm e_xt u_ready u_stat cn_mv cn_var cn_rstd cn_mask cn_coef v_ready
            f_mm x2_ready ln2_stat ln2_mv ln2_var ln2_rstd ln2_coef xs2_ready g_mm xt_hi_set xt_lo_set
            z_mm th_ready z_used h_hi h_lo acc_mm acc_ready
            rt_mm rt_copy rt_sum rt_max rt_idx rt_idx2 rt_gap rt_exp rt_den rt_g1 rt_g2 rt_eq rt_sel rt_gate
            gates_hi gates_ready
            w2_in w2_tr w2_copy acs_set fin_mm fin_ready row_in fin_out""".split()
        sm = {n: sem(n) for n in names}

        xd = a["x"].rearrange("q (h p) t -> q p h t", p=P)
        yd = a["ctx"].rearrange("q (h p) t -> q p h t", p=P)
        od = out.rearrange("q (h p) t -> q p h t", p=P)
        wn = ub[:, 0, :].rearrange("p (w n) -> p w n", w=8)
        ws = ub[:, 1, :].rearrange("p (w n) -> p w n", w=8)
        msk = act_t[:, 0, 0:P]
        mskc = act_t[0:NB * CT, 0, P:2 * P]
        vrow = act_t[0:6, 0, 2 * P:3 * P]
        vcol = act_t[:, 1, 0:6]
        graw = act_t[:, 1, 8:10]

        block = ctx.enter_context(nc.Block())

        @block.sync
        def _(sp):
            def load_x(j):
                for b in range(2):
                    need(sp, out_done[b], 16 * j)
                    need(sp, sm["xs2_ready"], 2 * j + b - 1)
                    sp.dma_start(xa[b], xd[2 * j + b]).then_inc(x_in[b], 16)

            def load_y(q):
                need(sp, sm["qk_mm"], CT * q)
                sp.dma_start(ya[:, :, :], yd[q]).then_inc(sm["y_in"], 16)

            def load_mask(q):
                need(sp, sm["xpre_ready"], q)
                sp.dma_start(mrow[:, :], a["mask"][q, 0, :].partition_broadcast(P)).then_inc(sm["mrow_in"], 16)

            def store(j):
                for b in range(2):
                    q = 2 * j + b
                    need(sp, sm["x2_ready"], 4 * q + 4)
                    sp.dma_start(od[q], xa[b]).then_inc(out_done[b], 16)

            def pair(j, last=False):
                load_x(j)
                for q in (2 * j + 1,) if last else (2 * j + 1, 2 * j + 2):
                    load_y(q)
                    load_mask(q)
                store(j)

            load_y(0)
            load_mask(0)
            pair(0)
            with sp.Fori(0, PAIRS - 2) as i:
                pair(i + 1)
            pair(PAIRS - 1, last=True)
            for b in range(2):
                sp.wait_ge(out_done[b], 16 * PAIRS)
            sp.wait_ge(sm["g_mm"], 4 * NB)
            sp.dma_start(w2st, a["w2"].rearrange("(f p) d -> p f d", p=P)).then_inc(sm["w2_in"], 16)
            sp.dma_start(wrs, out[0, 0:NE, :]).then_inc(sm["row_in"], 16)
            sp.wait_ge(sm["fin_ready"], 2)
            sp.dma_start(out[0, 0:NE, :], out8).then_inc(sm["fin_out"], 16)
            sp.wait_ge(sm["fin_out"], 16)

        @block.gpsimd
        def _(pool):
            pool.memset(ident[:, :], 0.0)
            pool.memset(nhalf[:, :], -0.5)
            pool.memset(minus[:, :], -1.0)
            pool.memset(sc[:, :, :], 0.0).then_inc(sm["sc_zero"], 1)
            pool.memset(sblk[:, :, :, :], 0.0)
            pool.memset(acc[:, :, :], 0.0).then_inc(sm["acc_ready"], 1)
            pool.memset(bv_b[:, :, :], 1.0)
            pool.iota(iot[:, :], pattern=[[1, NE]], base=0, channel_multiplier=0,
                      allow_small_or_imprecise_dtypes=True).then_inc(sm["s_zero"], 1)
            pool.wait_ge(sm["s_zero"], 1)
            pool.affine_select(out=ident[:, :], in_=ident[:, :], compare_op=ALU.not_equal, fill=1.0,
                               base=0, pattern=[[-1, P]], channel_multiplier=1).then_inc(sm["ident_set"], 1)

            def coefs(q, mvt, cot, n, eps, scale, what, used, mask=None):
                s_mv, s_var, s_rstd, s_coef = (sm[what + x] for x in ("_mv", "_var", "_rstd", "_coef"))
                pool.wait_ge(s_mv, q + 1)
                if used is not None:
                    need(pool, *used)
                pool.tensor_tensor(cot[:, 1, 0:n], mvt[:, 0:n, 0], minus[:, 0:n], ALU.mult)
                pool.tensor_scalar(cot[:, 0, 0:n], mvt[:, 0:n, 1], eps, scale ** -2, ALU.add, ALU.mult)\
                    .then_inc(s_var, 1)
                pool.wait_ge(s_var, q + 1)
                if mask is None:
                    pool.tensor_tensor(cot[:, 2, 0:n], cot[:, 0, 0:n], nhalf[:, 0:n], ALU.pow).then_inc(s_rstd, 1)
                else:
                    pool.tensor_tensor(cot[:, 4, 0:n], cot[:, 0, 0:n], nhalf[:, 0:n], ALU.pow)\
                        .then_inc(sm["cn_mask"], 1)
                    pool.wait_ge(sm["cn_mask"], q + 1)
                    pool.tensor_tensor(cot[:, 2, 0:n], cot[:, 4, 0:n], mask, ALU.mult).then_inc(s_rstd, 1)
                pool.wait_ge(s_rstd, q + 1)
                pool.tensor_tensor(cot[:, 3, 0:n], cot[:, 1, 0:n], cot[:, 2, 0:n], ALU.mult).then_inc(s_coef, 1)

            def largest(n, k):
                pool.wait_ge(sm["w_max"], n + 1)
                pool.partition_all_reduce(sc[:, k, 1:2], sc[:, k, 0:1], P, RMAX).then_inc(sm["w_all"], 1)

            coefs(0, mvc, coc, 8, EPS, 1.0, "ws", None)
            largest(0, 2)

            def attention(j, s):
                b, q = s % 2, 2 * j + s % 2
                if s in (0, 1):
                    coefs(q, mv, co, CH, EPS, XS, "ln1", (sm["xs_ready"], q))
                if s in (2, 3):
                    pool.wait_ge(sm["xhi_ready"], q + 1)
                    pool.tensor_tensor(x_lo[:, b], xs[b], x_hi[:, b], ALU.subtract).then_inc(sm["xlo_ready"], 1)
                if s in (4, 5):
                    for n in range(4):
                        c, h = n // 2, slice(TC * (n % 2), TC * (n % 2) + TC)
                        if n == 0:
                            pool.wait_ge(sm["mrow_in"], 16 * (q + 1))
                            pool.wait_ge(sm["gcol_set"], 1)
                            need(pool, sm["xpre_ready"], q)
                        else:
                            pool.wait_ge(sm["mtmp_step"], 7 * q + 2 * n)
                        pool.tensor_tensor(mtmp[:, :], mrow[:, h], gcol[:, 1, c:c + 1].broadcast_to([P, TC]), ALU.mult)\
                            .then_inc(sm["mtmp_step"], 1)
                        pool.wait_ge(sm["mtmp_step"], 7 * q + 2 * n + 1)
                        pool.tensor_tensor(xa[b][:, c, h], xa[b][:, c, h], mtmp[:, :], ALU.add)\
                            .then_inc(sm["mtmp_step" if n < 3 else "xpre_ready"], 1)
                if s in (8, 9):
                    coefs(q, mvc, coc, TT, EPS * XS * XS, 1.0, "cn", (sm["v_ready"], TT * q), m1c[:, b, :])
                if s in (10, 11):
                    coefs(q, mv2, co2, CH, EPS, XS, "ln2", (sm["xs2_ready"], q))

            for s in range(STAGES):
                if s in W_MAX:
                    largest(1 + W_MAX.index(s), 1 - W_MAX.index(s))
                attention(0, s)
            with pool.Fori(0, PAIRS - 1) as i:
                for s in range(STAGES):
                    attention(i + 1, s)

        @block.tensor
        def _(pe):
            def prepare():
                pe.wait_ge(sm["ident_set"], 1)
                pe.wait_ge(sm["small_in"], SMALL)
                pe.transpose(fbk[0][:, 0:P], msk, ident[:, :])
                pe.transpose(fbk[0][:, P:P + NB * CT], mskc, ident[0:NB * CT, 0:NB * CT])
                pe.transpose(fbk[0][:, 2 * P:2 * P + 6], vrow, ident[0:6, 0:6]).then_inc(sm["mask_tr"], 1)
                for d in range(FT):
                    last = pe.transpose(fbk[1][:, NE * d:NE * d + NE], wrs[:, P * d:P * d + P], ident[0:NE, 0:NE])
                last.then_inc(sm["wr_tr"], 1)
                pe.wait_ge(sm["ws_norm"], 8)
                for n in range(3):
                    for r in range(4):
                        w, o, c = (r // 2, r % 2, n) if n < 2 else (3, r % 2, r // 2)
                        last = pe.transpose(att[n][:, P * r:P * r + P], ws[:, 2 * w + o, P * c:P * c + P], ident[:, :])
                    last.then_inc(sm["ws_tr"], 1)
                pe.wait_ge(sm["ws_copy"], 3)

            def weight(s):
                for i in range(4 * (s - W_TR[0]), 4 * (s - W_TR[0]) + 4):
                    src, n = (w3n, w1n)[i // 16], i % 16
                    if i == 0:
                        pe.wait_ge(sm["w3_in"], 16)
                        pe.wait_ge(sm["mask_copy"], 1)
                        pe.wait_ge(sm["wr_lo"], 1)
                    if i == 16:
                        pe.wait_ge(sm["w1_in"], 16)
                    need(pe, sm["w_lo"], i - 3)
                    for r in range(4):
                        last = pe.transpose(wbk[i % 4][:, P * r:P * r + P],
                                            src[:, 4 * (n % 2) + r, P * (n // 2):P * (n // 2) + P], ident[:, :])
                    last.then_inc(sm["w_tr"], 1)

            def project(q, b, t):
                if t == 0:
                    pe.wait_ge(sm["y_in"], 16 * (q + 1))
                if t >= 2 or b == 1:
                    need(pe, sm["qk_evac"], CT * q + t - 1)
                else:
                    need(pe, sm["xt_lo_set"], 4 * q - 1 + t)
                for c in range(CH):
                    mm = pe.matmul(att[t % 2][:, :], ya[:, c, P * t:P * t + P], wqk[:, c, :],
                                   start=c == 0, stop=c == CH - 1)
                mm.then_inc(sm["qk_mm"], 1)

            def scores(q, b):
                pe.wait_ge(sm["q_ready"], CT * (q + 1))
                need(pe, *((sm["x2_ready"], 4 * q - 1) if b == 0 else (sm["sm_copy"], q)))
                for g in range(CH):
                    for t in range(CT):
                        mm = pe.matmul(att[2][:, P * g:P * g + P], qk[b][:, t, P * g:P * g + P],
                                       qk[b][:, t, S + P * g:S + P * g + P], start=t == 0, stop=t == CT - 1)
                mm.then_inc(sm["sc_mm"], 1)

            def out_times_scores(q, b):
                pe.wait_ge(sm["s_ready"], q + 1)
                need(pe, *((sm["x2_ready"], 4 * q) if b == 0 else (sm["cb_evac"], q)))
                for g in range(CH):
                    mm = pe.matmul(att[3][:, S * g:S * g + S], sblk[:, b, g, :], wo_t[:, g, :], start=True, stop=True)
                mm.then_inc(sm["t1_mm"], 1)

            def times_value(q, b):
                pe.wait_ge(sm["t1_evac"], q + 1)
                need(pe, *((sm["sm_copy"], q + 2) if b == 0 else (sm["mt_lo"], q)))
                for c in range(CH):
                    for g in range(CH):
                        mm = pe.matmul(att[2][:, S * c:S * c + S], wv_n[:, g, P * c:P * c + P], t1[:, g, :],
                                       start=g == 0, stop=g == CH - 1)
                mm.then_inc(sm["mt_mm"], 1)
                for g in range(CH):
                    mm = pe.matmul(att[3][:, 0:S], bv_b[:, g, :], t1[:, g, :], start=g == 0, stop=g == CH - 1)
                mm.then_inc(sm["cb_mm"], 1)

            def long_product(q, b, t):
                if t == 0:
                    pe.wait_ge(sm["xlo_ready"], q + 1)
                    pe.wait_ge(sm["mt_lo"], q + 1)
                if t >= 2 or b == 1:
                    need(pe, sm["u_ready"], TT * q + t - 1)
                else:
                    need(pe, sm["qk_evac"], CT * (q + 1) + 3 + t)
                bk = att[t % 2]
                for c in range(CH):
                    pe.transpose(bk[:, P * c:P * c + P], xs[b][:, c, P * t:P * t + P], ident[:, :])
                n = 0
                for c in range(CH):
                    for left, right in ((x_hi, m_hi), (x_hi, m_lo), (x_lo, m_hi)):
                        mm = pe.matmul(bk[:, S:2 * S], left[:, b, c, P * t:P * t + P], right[:, b, c, :],
                                       start=n == 0, stop=n == 5)
                        n += 1
                mm.then_inc(sm["e_mm"], 1)

            def attention_back(q, b, n):
                pe.wait_ge(sm["v_ready"], TT * q + 4 * (n % 2) + 4)
                if n >= 2 or b == 1:
                    need(pe, sm["x2_ready"], 4 * q + n - 1)
                else:
                    need(pe, sm["mt_lo" if n == 0 else "cb_evac"], q + 2)
                for r in range(4):
                    mm = pe.transpose(att[2 + n % 2][:, P * r:P * r + P],
                                      u[b][:, 4 * (n % 2) + r, P * (n // 2):P * (n // 2) + P], ident[:, :])
                mm.then_inc(sm["f_mm"], 1)

            def tokens_transposed(q, b, n):
                if n == 0:
                    pe.wait_ge(sm["xs2_ready"], q + 1)
                if n >= 2 or b == 1:
                    need(pe, sm["xt_lo_set"], 4 * q + n - 1)
                else:
                    need(pe, sm["u_ready"], TT * (q + 1) + 7 + n)
                for r in range(4):
                    t, c = 2 * n + r // 2, r % 2
                    mm = pe.transpose(att[n % 2][:, P * r:P * r + P], xs[b][:, c, P * t:P * t + P], ident[:, :])
                mm.then_inc(sm["g_mm"], 1)

            def attention(j, s, d):
                b = s % 2
                if s in (0, 2) and d % 2 == 0:
                    project(2 * j + s // 2, s // 2, d // 2)
                elif s in (1, 3) and d == 0:
                    scores(2 * j + s // 2, s // 2)
                elif s in (3, 5) and d == 4:
                    out_times_scores(2 * j + (s - 3) // 2, (s - 3) // 2)
                elif s in (4, 6) and d == 4:
                    times_value(2 * j + (s - 4) // 2, (s - 4) // 2)
                elif s in (8, 9):
                    long_product(2 * j + b, b, d)
                elif s in (10, 11) and d % 2 == 0:
                    attention_back(2 * j + b, b, d // 2)
                elif s in (12, 13) and d % 2 == 0:
                    tokens_transposed(2 * j + b, b, d // 2)

            def ffn(j, g, d):
                if g == GROUPS:
                    j, g = j + 1, 0
                bk = fbk[g % 2]
                if d == 0 and g == 0:
                    need(pe, sm["z_used"], GROUPS * j - 1)
                if d == 0 and g > 1:
                    need(pe, sm["z_used"], GROUPS * j + g - 1)
                if g < FT:
                    if g == 0 and d == 0:
                        pe.wait_ge(sm["xt_lo_set"], 8 * (j + 1))
                    f = slice(P * g, P * g + P)
                    parts = ((w1_hi[:, d, f], xt_hi[:, d, :]), (w1_hi[:, d, f], xt_lo[:, d, :]),
                             (w1_lo[:, d, f], xt_hi[:, d, :]))
                else:
                    if g == FT:
                        pe.wait_ge(sm["h_lo"], GROUPS * j + d + 1)
                    k, f = (g - FT) // 2, slice(TOK * (g % 2), TOK * (g % 2) + TOK)
                    tok = slice(P * k, P * k + P)
                    parts = ((h1_hi[:, d, tok], w3_hi[:, d, f]), (h1_hi[:, d, tok], w3_lo[:, d, f]),
                             (h1_lo[:, d, tok], w3_hi[:, d, f]))
                for n, (left, right) in enumerate(parts):
                    mm = pe.matmul(bk[:, :], left, right, start=d == 0 and n == 0, stop=d == FT - 1 and n == 2)
                if d == FT - 1:
                    mm.then_inc(sm["z_mm"], 1)

            def router(j):
                for k in range(KT):
                    for d in range(FT):
                        for n, x in enumerate((xt_hi, xt_lo)):
                            mm = pe.matmul(rbk[:, 16 * k:16 * k + 16], x[:, d, P * k:P * k + P], wr_t[:, d, :],
                                           start=d == 0 and n == 0, stop=d == FT - 1 and n == 1)
                mm.then_inc(sm["rt_mm"], 1)

            def gated_sum(j, g):
                pe.wait_ge(sm["h_lo"], GROUPS * j + g + 1)
                if g == FT:
                    pe.wait_ge(sm["gates_ready"], j + 1)
                    pe.wait_ge(sm["acc_ready"], j + 1)
                k = (g - FT) // 2
                for m in range(4):
                    blk = 4 * (g % 2) + m
                    for n, h in enumerate((h2_hi, h2_lo)):
                        mm = pe.matmul(abk[:, 16 * blk:16 * blk + 16], h[:, g % 2, P * m:P * m + P], gts[:, k, :],
                                       start=g == FT and m == 0 and n == 0, stop=g == GROUPS - 1 and m == 3 and n == 1,
                                       skip_group_check=True)
                mm.then_inc(sm["acc_mm"], 1)

            def value_out(n):
                k, h = n // 2, n % 2
                if n == 0:
                    pe.wait_ge(sm["w2_in"], 16)
                need(pe, sm["w2_copy"], n - 3)
                for r in range(4):
                    mm = pe.transpose(att[n % 4][:, P * r:P * r + P], w2st[:, 4 * h + r, P * k:P * k + P], ident[:, :])
                mm.then_inc(sm["w2_tr"], 1)

            def group(j, g, ja=None):
                for d in range(FT):
                    if ja is not None:
                        attention(ja, g - 1, d)
                    ffn(j, g, d)
                if g == 1:
                    router(j)
                if g > FT:
                    gated_sum(j, g - 1)

            prepare()
            for s in range(STAGES):
                for d in range(FT):
                    attention(0, s, d)
                if s in W_TR:
                    weight(s)
            pe.wait_ge(sm["w_lo"], 32)
            group(0, 0)
            with pe.Fori(0, PAIRS - 1) as i:
                for g in range(1, GROUPS + 1):
                    group(i, g, i + 1)
            for g in range(1, GROUPS):
                group(PAIRS - 1, g)
                if g >= FT:
                    value_out(2 * (g - FT))
                    value_out(2 * (g - FT) + 1)
            gated_sum(PAIRS - 1, GROUPS - 1)

            pe.wait_ge(sm["acs_set"], 1)
            pe.wait_ge(sm["w2_copy"], 2 * FT)
            for h in range(2):
                for k in range(FT):
                    mm = pe.matmul(fbk[h][0:NE, :], acs[:, k, :], w2t[:, k, 512 * h:512 * h + 512],
                                   start=k == 0, stop=k == FT - 1)
                mm.then_inc(sm["fin_mm"], 1)

        @block.scalar
        def _(act):
            smalls = [(wn[:, 2 * n:2 * n + 2, :], a[w].rearrange("(c p) n -> p c n", p=P))
                      for n, w in enumerate(("wq", "wk", "wv", "wo"))]
            smalls += [(wrs, a["wr"]), (msk, a["mask"].rearrange("q o (t p) -> (q o t) p", p=P)),
                       (mskc, a["mask_cond"].rearrange("q o (t p) -> (q o t) p", p=P)),
                       (qkb_b[:, 0:S], a["bq"].partition_broadcast(P)), (qkb_b[:, S:2 * S], a["bk"].partition_broadcast(P)),
                       (bo_b[:, :], a["bo"].partition_broadcast(P)),
                       (vrow[0:2, :], a["bv"].rearrange("(c p) -> c p", p=P)),
                       (vrow[2:4, :], a["gamma"].rearrange("(c p) -> c p", p=P)),
                       (vrow[4:6, :], a["beta"].rearrange("(c p) -> c p", p=P)),
                       (graw[:, 0:1], a["g_xattn"].partition_broadcast(P)),
                       (graw[:, 1:2], a["g_ffn"].partition_broadcast(P))]
            assert SMALL == 16 * len(smalls)
            for dst, src in smalls:
                act.dma_start(dst, src).then_inc(sm["small_in"], 16)
            act.dma_start(w3n, a["w3"].rearrange("(f p) d -> p f d", p=P)).then_inc(sm["w3_in"], 16)
            act.dma_start(w1n, a["w1"].rearrange("(f p) d -> p f d", p=P)).then_inc(sm["w1_in"], 16)
            act.wait_ge(sm["small_in"], SMALL)
            act.activation(tg[:, :], graw, ACT.Tanh).then_inc(sm["tg_set"], 1)
            act.wait_ge(sm["ws_coef"], 1)
            for n in range(8):
                dst = wv_n[:, n - 4, :] if n in (4, 5) else ws[:, n, :]
                act.activation(dst, wn[:, n, :], ACT.Identity, bias=coc[:, 3, n:n + 1], scale=coc[:, 2, n:n + 1])\
                    .then_inc(sm["ws_norm"], 1)
            for n in range(3):
                act.wait_ge(sm["ws_tr"], n + 1)
                dst = wqk[:, n, :] if n < 2 else wo_t[:, :, :]
                src = att[n][:, :] if n < 2 else att[n][:, :].rearrange("p (c n) -> p c n", c=CH)
                act.activation(dst, src, ACT.Copy).then_inc(sm["ws_copy"], 1)
            act.wait_ge(sm["w_scale"], 1)
            act.wait_ge(sm["wr_tr"], 1)
            act.activation(wr_t[:, :, 0:NE], fbk[1][:, 0:FT * NE].rearrange("p (d n) -> p d n", d=FT), ACT.Copy,
                           scale=sc[:, 2, 2:3]).then_inc(sm["wr_hi"], 1)

            def weight(s):
                for i in range(4 * (s - W_TR[0]), 4 * (s - W_TR[0]) + 4):
                    dst, n, k = (w3_hi, w1_hi)[i // 16], i % 16, 1 - i // 16
                    if n == 0:
                        act.wait_ge(sm["w_scale"], 2 + i // 16)
                    act.wait_ge(sm["w_tr"], i + 1)
                    act.activation(dst[:, n // 2, 512 * (n % 2):512 * (n % 2) + 512], wbk[i % 4][:, :], ACT.Copy,
                                   scale=sc[:, k, 2:3]).then_inc(sm["w_hi"], 1)

            def normed(q, b, c_, s_coef, s_done):
                act.wait_ge(s_coef, q + 1)
                for c in range(CH):
                    ins = act.activation(xs[b][:, c, :], xa[b][:, c, :], ACT.Identity,
                                         bias=c_[:, 3, c:c + 1], scale=c_[:, 2, c:c + 1])
                ins.then_inc(s_done, 1)

            def attention(j, s):
                b, q = s % 2, 2 * j + s % 2
                if s in (0, 1):
                    normed(q, b, co, sm["ln1_coef"], sm["xs_ready"])
                if s in (0, 2):
                    b, q = s // 2, 2 * j + s // 2
                    for t in range(CT):
                        act.wait_ge(sm["qk_evac"], CT * q + t + 1)
                        act.activation(qk[b][:, t, 0:S], qk[b][:, t, 0:S], ACT.Copy, scale=mcc[:, b, t:t + 1])\
                            .then_inc(sm["q_ready"], 1)
                if s in (1, 3):
                    q = 2 * j + s // 2
                    act.wait_ge(sm["sm_sub"], q + 1)
                    act.activation(dg[:, :, :], dg[:, :, :], ACT.Exp, scale=SCORE).then_inc(sm["sm_exp"], 1)
                if s in (3, 5):
                    q = 2 * j + (s - 3) // 2
                    act.wait_ge(sm["t1_mm"], q + 1)
                    act.activation(t1[:, :, :], att[3][:, :].rearrange("p (c n) -> p c n", c=CH), ACT.Copy)\
                        .then_inc(sm["t1_evac"], 1)
                if s in (4, 6):
                    b, q = (s - 4) // 2, 2 * j + (s - 4) // 2
                    for t in range(TT):
                        ins = act.activation(u[b][:, t, :], bo_b[:, :], ACT.Copy, scale=m1c[:, b, t:t + 1])
                    ins.then_inc(sm["ub_part"], 1)
                    act.wait_ge(sm["mt_mm"], q + 1)
                    act.activation(m_hi[:, b], att[2][:, :].rearrange("p (c n) -> p c n", c=CH), ACT.Copy, scale=MS)\
                        .then_inc(sm["mt_hi"], 1)
                    act.wait_ge(sm["cb_mm"], q + 1)
                    act.activation(cb[:, b, :], att[3][:, 0:S], ACT.Copy, scale=XS).then_inc(sm["cb_evac"], 1)
                if s in (9, 10):
                    b, q = s - 9, 2 * j + s - 9
                    act.wait_ge(sm["cn_coef"], q + 1)
                    for t in range(TT):
                        act.activation(u[b][:, t, :], u[b][:, t, :], ACT.Identity, bias=coc[:, 3, t:t + 1],
                                       scale=coc[:, 2, t:t + 1]).then_inc(sm["v_ready"], 1)
                if s in (11, 12):
                    normed(2 * j + s - 11, s - 11, co2, sm["ln2_coef"], sm["xs2_ready"])
                if s in (12, 13):
                    b, q = s - 12, 2 * j + s - 12
                    for n in range(4):
                        act.wait_ge(sm["g_mm"], 4 * q + n + 1)
                        act.activation(xt_hi[:, 2 * n:2 * n + 2, S * b:S * b + S],
                                       att[n % 2][:, :].rearrange("p (t n) -> p t n", t=2), ACT.Copy)\
                            .then_inc(sm["xt_hi_set"], 1)

            def ffn(j, g):
                first = g % GROUPS < FT
                act.wait_ge(sm["z_mm"], GROUPS * j + g + 1)
                act.activation(act_t[:, g % 2, :], fbk[g % 2][:, :], ACT.Tanh,
                               scale=fs[:, 0:1] if first else fs[:, 1:2]).then_inc(sm["th_ready"], 1)
                if FT + 2 <= g < GROUPS:
                    act.wait_ge(sm["acc_mm"], 8 * j + g - FT - 1)
                act.wait_ge(sm["z_used"], GROUPS * j + g + 1)
                act.activation(h1_hi[:, g % GROUPS, :] if first else h2_hi[:, g % 2, :], act_t[:, g % 2, :], ACT.Copy,
                               scale=H1S if first else H2S).then_inc(sm["h_hi"], 1)

            def gates(j):
                act.wait_ge(sm["rt_gap"], j + 1)
                act.activation(gd[:, 1, :], gd[:, 0, :], ACT.Exp, scale=fs[:, 2:3]).then_inc(sm["rt_exp"], 1)

            def group(j, g, ja=None):
                if ja is not None:
                    attention(ja, g - 1)
                ffn(j, g)
                if g == 5:
                    gates(j)

            for s in range(STAGES):
                attention(0, s)
                if s in W_TR:
                    weight(s)
            act.wait_ge(sm["fs_set"], 1)
            group(0, 0)
            with act.Fori(0, PAIRS - 1) as i:
                for g in range(1, GROUPS + 1):
                    group(i, g, i + 1)
            for g in range(1, GROUPS):
                group(PAIRS - 1, g)
                if g >= FT:
                    for n in (2 * (g - FT), 2 * (g - FT) + 1):
                        act.wait_ge(sm["w2_tr"], n + 1)
                        at = slice(512 * (n % 2), 512 * (n % 2) + 512)
                        act.activation(w2t[:, n // 2, at], att[n % 4][:, :], ACT.Copy).then_inc(sm["w2_copy"], 1)

        @block.vector
        def _(dve):
            def carry():
                dve.memset(spare[:, :], 0.0)

            def scale_of(n, k, src, parts):
                dve.tensor_reduce(sc[0:parts, k, 0:1], src, AX.XY if parts == P else AX.X, ALU.max,
                                  apply_absolute_value=True).then_inc(sm["w_max"], 1)
                dve.wait_ge(sm["w_all"], n + 1)
                dve.tensor_scalar(sc[:, k, 0:1], sc[:, k, 1:2], 1e-30, None, ALU.max).then_inc(sm["w_clamp"], 1)
                dve.wait_ge(sm["w_clamp"], n + 1)
                si = sc[:, k, :].bitcast(I32)
                dve.tensor_scalar(si[:, 0:1], si[:, 0:1], 0x7F800000, None, ALU.bitwise_and)\
                    .then_inc(sm["w_bits"], 1)
                dve.wait_ge(sm["w_bits"], n + 1)
                dve.tensor_scalar(si[:, 2:3], si[:, 0:1], -1.0, float(268 << 23), ALU.mult, ALU.add)
                dve.tensor_scalar(si[:, 3:4], si[:, 0:1], -float(14 << 23), None, ALU.add)\
                    .then_inc(sm["w_scale"], 1)
                dve.wait_ge(sm["w_scale"], n + 1)

            def prepare():
                dve.wait_ge(sm["small_in"], SMALL)
                for n in range(8):
                    ins = dve.bn_stats(bst[:, n, :], wn[:, n, :])
                ins.then_inc(sm["ws_stat"], 1)
                dve.wait_ge(sm["ws_stat"], 1)
                for n in range(8):
                    ins = dve.bn_aggr(mvc[:, n, :], bst[:, n, :])
                ins.then_inc(sm["ws_mv"], 1)
                dve.wait_ge(sm["mask_tr"], 1)
                dve.tensor_copy(vcol, fbk[0][:, 2 * P:2 * P + 6])
                dve.tensor_copy(mtab[:, :, 0:16], fbk[0][:, 0:P].rearrange("p (j n) -> p j n", j=PAIRS))
                dve.tensor_copy(mtab[:, :, 48:56], fbk[0][:, P:P + 64].rearrange("p (j n) -> p j n", j=PAIRS))\
                    .then_inc(sm["mask_copy"], 1)
                dve.wait_ge(sm["mask_copy"], 1)
                dve.tensor_tensor(mtab[:, :, 16:32], mtab[:, :, 0:16], mtab[:, :, 0:16], ALU.mult)
                dve.tensor_tensor(mtab[:, :, 48:56], mtab[:, :, 48:56], mtab[:, :, 48:56], ALU.mult)\
                    .then_inc(sm["mask_sq"], 1)
                dve.wait_ge(sm["mask_sq"], 1)
                dve.tensor_scalar(mtab[:, :, 32:48], mtab[:, :, 16:32], 1.0 / MS, None, ALU.mult)\
                    .then_inc(sm["mask_sq"], 1)
                dve.wait_ge(sm["mask_sq"], 2)
                dve.wait_ge(sm["tg_set"], 1)
                dve.tensor_scalar(gcol[:, :, :], vcol[:, 2:6].rearrange("p (a c) -> p a c", a=2), tg[:, 0:1], None, ALU.mult).then_inc(sm["gcol_set"], 1)
                dve.tensor_scalar(bo_b[:, :], bo_b[:, :], XS, None, ALU.mult)
                dve.wait_ge(sm["s_zero"], 1)
                for g in range(CH):
                    ins = dve.tensor_scalar(bv_b[:, g, :], bv_b[:, g, :], vcol[:, g:g + 1], None, ALU.mult)
                ins.then_inc(sm["bias_set"], 1)
                dve.wait_ge(sm["bias_set"], 1)
                dve.wait_ge(sm["sc_zero"], 1)

                scale_of(0, 2, wrs, NE)
                dve.wait_ge(sm["wr_hi"], 1)
                dve.scalar_tensor_tensor(out=wr_t[:, :, NE:2 * NE], in0=fbk[1][:, 0:FT * NE].rearrange("p (d n) -> p d n", d=FT),
                                         scalar=sc[:, 2, 2:3], in1=wr_t[:, :, 0:NE], op0=ALU.mult, op1=ALU.subtract)\
                    .then_inc(sm["wr_lo"], 1)

            def largest(i):
                dve.wait_ge(sm[("w3_in", "w1_in")[i]], 16)
                scale_of(1 + i, 1 - i, (w3n, w1n)[i], P)

            def weight(s):
                for i in range(4 * (s - W_TR[0]), 4 * (s - W_TR[0]) + 4):
                    (hi, lo), n, k = ((w3_hi, w3_lo), (w1_hi, w1_lo))[i // 16], i % 16, 1 - i // 16
                    at = slice(512 * (n % 2), 512 * (n % 2) + 512)
                    dve.wait_ge(sm["w_hi"], i + 1)
                    dve.scalar_tensor_tensor(out=lo[:, n // 2, at], in0=wbk[i % 4][:, :], scalar=sc[:, k, 2:3],
                                             in1=hi[:, n // 2, at], op0=ALU.mult, op1=ALU.subtract)\
                        .then_inc(sm["w_lo"], 1)

            def final_scales():
                dve.tensor_scalar(fs[:, 0:1], sc[:, 0, 3:4], 2.0 ** -11, None, ALU.mult)
                dve.tensor_scalar(fs[:, 2:3], sc[:, 2, 3:4], 1.0 / XS, None, ALU.mult)
                dve.tensor_scalar(fs[:, 1:2], sc[:, 0, 3:4], sc[:, 1, 3:4], 2.0 ** 9, ALU.mult, ALU.mult)\
                    .then_inc(sm["fs_part"], 1)
                dve.wait_ge(sm["fs_part"], 1)
                dve.tensor_scalar(fs[:, 3:4], fs[:, 1:2], tg[:, 1:2], 2.0 ** 26, ALU.mult, ALU.mult)\
                    .then_inc(sm["fs_set"], 1)

            def ln1(j, b):
                q = 2 * j + b
                dve.wait_ge(x_in[b], 16 * (j + 1))
                for n in range(4):
                    ins = dve.bn_stats(bst[:, n, :], xa[b][:, n // 2, TC * (n % 2):TC * (n % 2) + TC])
                ins.then_inc(sm["ln1_stat"], 1)
                dve.wait_ge(sm["ln1_stat"], q + 1)
                need(dve, sm["ln1_coef"], q)
                carry()
                for c in range(CH):
                    ins = dve.bn_aggr(mv[:, c, :], bst[:, 2 * c:2 * c + 2, :])
                ins.then_inc(sm["ln1_mv"], 1)

            def x_high(q, b):
                dve.wait_ge(sm["xs_ready"], q + 1)
                dve.tensor_copy(x_hi[:, b], xs[b]).then_inc(sm["xhi_ready"], 1)

            def softmax(q, b):
                dve.wait_ge(sm["sc_mm"], q + 1)
                for h in range(4):
                    r = slice(HD * h, HD * h + HD)
                    ins = dve.tensor_copy(dg[r, :, :], att[2][r, 0:2 * P].rearrange("p (g n) -> p g n", g=CH)[:, :, r])
                ins.then_inc(sm["sm_copy"], 1)
                dve.wait_ge(sm["sm_copy"], q + 1)
                dve.tensor_reduce(dr[:, 0, :], dg[:, :, :], AX.X, ALU.max).then_inc(sm["sm_max"], 1)
                dve.wait_ge(sm["sm_max"], q + 1)
                dve.tensor_tensor(dg[:, :, :], dg[:, :, :], dr[:, 0, :].unsqueeze(2).broadcast_to([P, CH, HD]),
                                  ALU.subtract).then_inc(sm["sm_sub"], 1)
                dve.wait_ge(sm["sm_exp"], q + 1)
                dve.tensor_reduce(dr[:, 1, :], dg[:, :, :], AX.X, ALU.add).then_inc(sm["sm_sum"], 1)
                dve.wait_ge(sm["sm_sum"], q + 1)
                dve.reciprocal(dr[:, 2, :], dr[:, 1, :]).then_inc(sm["sm_rec"], 1)
                dve.wait_ge(sm["sm_rec"], q + 1)
                for h in range(4):
                    r = slice(HD * h, HD * h + HD)
                    ins = dve.tensor_tensor(sblk[r, b, :, r], dg[r, :, :],
                                            dr[r, 2, :].unsqueeze(2).broadcast_to([HD, CH, HD]), ALU.mult)
                ins.then_inc(sm["s_ready"], 1)

            def bias_tiles(q, b):
                dve.wait_ge(sm["ub_part"], q + 1)
                dve.wait_ge(sm["cb_evac"], q + 1)
                for t in range(TT):
                    ins = dve.scalar_tensor_tensor(out=u[b][:, t, :], in0=cb[:, b, :], scalar=m2c[:, b, t:t + 1],
                                                   in1=u[b][:, t, :], op0=ALU.mult, op1=ALU.add)
                ins.then_inc(sm["ub_ready"], 1)

            def attention_out(q, b):
                dve.wait_ge(sm["ub_ready"], q + 1)

                def stats(t):
                    dve.wait_ge(sm["u_ready"], TT * q + t + 1)
                    dve.bn_stats(bst2[:, t, :], u[b][:, t, :]).then_inc(sm["u_stat"], 1)

                for t in range(TT):
                    bk = att[t % 2]
                    dve.wait_ge(sm["e_mm"], TT * q + t + 1)
                    dve.tensor_tensor(u[b][:, t, :], u[b][:, t, :], bk[:, 0:S], ALU.add).then_inc(sm["e_xt"], 1)
                    if t > 0:
                        stats(t - 1)
                    dve.wait_ge(sm["e_xt"], TT * q + t + 1)
                    dve.scalar_tensor_tensor(out=u[b][:, t, :], in0=bk[:, S:2 * S], scalar=m2s[:, b, t:t + 1],
                                             in1=u[b][:, t, :], op0=ALU.mult, op1=ALU.add).then_inc(sm["u_ready"], 1)
                stats(TT - 1)
                dve.wait_ge(sm["u_stat"], TT * (q + 1))
                need(dve, sm["cn_coef"], q)
                carry()
                for t in range(TT):
                    ins = dve.bn_aggr(mvc[:, t, :], bst2[:, t, :])
                ins.then_inc(sm["cn_mv"], 1)

            def residual(q, b):
                dve.wait_ge(sm["xpre_ready"], q + 1)

                def stats(n):
                    dve.wait_ge(sm["x2_ready"], 4 * q + n + 1)
                    dve.bn_stats(bst[:, n, :], xa[b][:, n // 2, TC * (n % 2):TC * (n % 2) + TC])\
                        .then_inc(sm["ln2_stat"], 1)

                for n in range(4):
                    c, h = n // 2, slice(TC * (n % 2), TC * (n % 2) + TC)
                    dve.wait_ge(sm["f_mm"], 4 * q + n + 1)
                    dve.scalar_tensor_tensor(out=xa[b][:, c, h], in0=att[2 + n % 2][:, :], scalar=gcol[:, 0, c:c + 1],
                                             in1=xa[b][:, c, h], op0=ALU.mult, op1=ALU.add).then_inc(sm["x2_ready"], 1)
                    if n > 0:
                        stats(n - 1)
                stats(3)
                dve.wait_ge(sm["ln2_stat"], 4 * (q + 1))
                need(dve, sm["ln2_coef"], q)
                carry()
                for c in range(CH):
                    ins = dve.bn_aggr(mv2[:, c, :], bst[:, 2 * c:2 * c + 2, :])
                ins.then_inc(sm["ln2_mv"], 1)

            def attention(j, s):
                if s == 0:
                    need(dve, sm["cn_coef"], 2 * j)
                    need(dve, sm["q_ready"], 2 * CT * j)
                    dve.tensor_copy(mcur[:, :], mtab[:, j, :]).then_inc(sm["mcur_set"], 1)
                    dve.wait_ge(sm["mcur_set"], j + 1)
                if s in (0, 1):
                    ln1(j, s)
                if s in (0, 2):
                    b, q = s // 2, 2 * j + s // 2
                    for t in range(CT):
                        dve.wait_ge(sm["qk_mm"], CT * q + t + 1)
                        dve.tensor_tensor(qk[b][:, t, :], att[t % 2][:, :], qkb_b[:, :], ALU.add)\
                            .then_inc(sm["qk_evac"], 1)
                if s in (1, 3):
                    softmax(2 * j + s // 2, s // 2)
                if s in (1, 2):
                    x_high(2 * j + s - 1, s - 1)
                if s in (5, 7):
                    bias_tiles(2 * j + (s - 5) // 2, (s - 5) // 2)
                if s in (4, 6):
                    b, q = (s - 4) // 2, 2 * j + (s - 4) // 2
                    dve.wait_ge(sm["mt_hi"], q + 1)
                    dve.scalar_tensor_tensor(out=m_lo[:, b], in0=att[2][:, :].rearrange("p (c n) -> p c n", c=CH), scalar=MS,
                                             in1=m_hi[:, b], op0=ALU.mult, op1=ALU.subtract).then_inc(sm["mt_lo"], 1)
                if s in (8, 9):
                    attention_out(2 * j + s - 8, s - 8)
                if s in (10, 11):
                    residual(2 * j + s - 10, s - 10)
                if s in (12, 13):
                    b, q = s - 12, 2 * j + s - 12
                    for n in range(4):
                        dve.wait_ge(sm["xt_hi_set"], 4 * q + n + 1)
                        dve.tensor_tensor(xt_lo[:, 2 * n:2 * n + 2, S * b:S * b + S],
                                          att[n % 2][:, :].rearrange("p (t n) -> p t n", t=2),
                                          xt_hi[:, 2 * n:2 * n + 2, S * b:S * b + S], ALU.subtract)\
                            .then_inc(sm["xt_lo_set"], 1)

            def ffn(j, g):
                buf, first = act_t[:, g % 2, :], g % GROUPS < FT
                dve.wait_ge(sm["th_ready"], GROUPS * j + g + 1)
                dve.scalar_tensor_tensor(out=buf, in0=buf, scalar=1.0, in1=fbk[g % 2][:, :], op0=ALU.add, op1=ALU.mult)\
                    .then_inc(sm["z_used"], 1)
                dve.wait_ge(sm["h_hi"], GROUPS * j + g + 1)
                hi = h1_hi[:, g % GROUPS, :] if first else h2_hi[:, g % 2, :]
                lo = h1_lo[:, g % GROUPS, :] if first else h2_lo[:, g % 2, :]
                dve.scalar_tensor_tensor(out=lo, in0=buf, scalar=H1S if first else H2S, in1=hi,
                                         op0=ALU.mult, op1=ALU.subtract).then_inc(sm["h_lo"], 1)

            def top_two(j):
                dve.wait_ge(sm["rt_mm"], j + 1)
                dve.tensor_copy(lg[:, :, :], rbk[:, 0:KT * 16].rearrange("p (k n) -> p k n", k=KT))\
                    .then_inc(sm["rt_copy"], 1)
                dve.wait_ge(sm["rt_copy"], j + 1)
                dve.tensor_tensor(lgs[:, :, :], lg[:, :, 0:NE], lg[:, :, NE:2 * NE], ALU.add).then_inc(sm["rt_sum"], 1)
                dve.wait_ge(sm["rt_sum"], j + 1)
                carry()
                for k in range(KT):
                    ins = dve.max(top[:, k, :], lgs[:, k, :])
                ins.then_inc(sm["rt_max"], 1)
                dve.wait_ge(sm["rt_max"], j + 1)
                dve.tensor_tensor(gd[:, 0, :], top[:, :, 1], top[:, :, 0], ALU.subtract).then_inc(sm["rt_gap"], 1)
                for k in range(KT):
                    ins = dve.max_index(topi[:, k, :], top[:, k, :], lgs[:, k, :])
                ins.then_inc(sm["rt_idx"], 1)
                dve.wait_ge(sm["rt_idx"], j + 1)
                dve.tensor_copy(topf[:, :, :], topi[:, :, 0:2]).then_inc(sm["rt_idx2"], 1)

            def gates(j):
                dve.wait_ge(sm["rt_exp"], j + 1)
                dve.tensor_scalar(gd[:, 0, :], gd[:, 1, :], 1.0, None, ALU.add).then_inc(sm["rt_den"], 1)
                dve.wait_ge(sm["rt_den"], j + 1)
                dve.reciprocal(gd[:, 2, :], gd[:, 0, :]).then_inc(sm["rt_g1"], 1)
                dve.wait_ge(sm["rt_idx2"], j + 1)
                for n, e in enumerate((e1t, e2t)):
                    ins = dve.tensor_tensor(e[:, :, :], iot[:, :].unsqueeze(1).broadcast_to([P, KT, NE]),
                                            topf[:, :, n].unsqueeze(2).broadcast_to([P, KT, NE]), ALU.is_equal)
                ins.then_inc(sm["rt_eq"], 1)
                dve.wait_ge(sm["rt_g1"], j + 1)
                dve.tensor_tensor(gd[:, 3, :], gd[:, 1, :], gd[:, 2, :], ALU.mult).then_inc(sm["rt_g2"], 1)
                dve.wait_ge(sm["rt_eq"], j + 1)
                dve.wait_ge(sm["rt_g2"], j + 1)
                for n, e in enumerate((e1t, e2t)):
                    ins = dve.tensor_tensor(e[:, :, :], e[:, :, :], gd[:, 2 + n, :].unsqueeze(2).broadcast_to([P, KT, NE]),
                                            ALU.mult)
                ins.then_inc(sm["rt_sel"], 1)
                dve.wait_ge(sm["rt_sel"], j + 1)
                dve.tensor_tensor(e1t[:, :, :], e1t[:, :, :], e2t[:, :, :], ALU.add).then_inc(sm["rt_gate"], 1)
                dve.wait_ge(sm["rt_gate"], j + 1)
                dve.tensor_copy(gts[:, :, 0:NE], e1t[:, :, :]).then_inc(sm["gates_hi"], 1)
                dve.wait_ge(sm["gates_hi"], j + 1)
                dve.tensor_tensor(gts[:, :, NE:2 * NE], e1t[:, :, :], gts[:, :, 0:NE], ALU.subtract)\
                    .then_inc(sm["gates_ready"], 1)

            def group(j, g, ja=None):
                if ja is not None:
                    attention(ja, g - 1)
                if g == 7:
                    gates(j)
                ffn(j, g)
                if g == 5:
                    top_two(j)

            def add_sums(j):
                dve.wait_ge(sm["acc_mm"], 8 * (j + 1))
                dve.wait_ge(sm["acc_ready"], j + 1)
                dve.tensor_tensor(acc[:, :, :], acc[:, :, :], abk[:, 0:P].rearrange("p (k n) -> p k n", k=FT),
                                  ALU.add).then_inc(sm["acc_ready"], 1)

            prepare()
            for s in range(STAGES):
                attention(0, s)
                if s in W_MAX:
                    largest(W_MAX.index(s))
                if s in W_TR:
                    weight(s)
            final_scales()
            group(0, 0)
            with dve.Fori(0, PAIRS - 1) as i:
                for g in range(1, GROUPS + 1):
                    group(i, g, i + 1)
                add_sums(i)
            for g in range(1, GROUPS):
                group(PAIRS - 1, g)
            add_sums(PAIRS - 1)

            dve.wait_ge(sm["acc_ready"], PAIRS + 1)
            dve.tensor_tensor(acs[:, :, :], acc[:, :, 0:NE], acc[:, :, NE:2 * NE], ALU.add).then_inc(sm["acs_set"], 1)
            dve.wait_ge(sm["row_in"], 16)
            for h in range(2):
                dve.wait_ge(sm["fin_mm"], h + 1)
                at = slice(512 * h, 512 * h + 512)
                dve.scalar_tensor_tensor(out=out8[:, at], in0=fbk[h][0:NE, :], scalar=fs[0:NE, 3:4], in1=wrs[:, at],
                                         op0=ALU.mult, op1=ALU.add).then_inc(sm["fin_ready"], 1)


_INS = {"x": "x", "ctx": "ctx_1024", "mask": "mask_Bx1x2048_ff1", "mask_cond": "mask_Bx1x1024_ff1",
        "g_xattn": "g_xattn", "g_ffn": "g_ffn",
        "wq": "L0_xattn_wq", "bq": "L0_xattn_bq", "wk": "L0_xattn_wk", "bk": "L0_xattn_bk",
        "wv": "L0_xattn_wv", "bv": "L0_xattn_bv", "wo": "L0_xattn_wo", "bo": "L0_xattn_bo",
        "gamma": "L0_xattn_gamma", "beta": "L0_xattn_beta",
        "w1": "L0_ffn_w1", "w3": "L0_ffn_w3", "w2": "L0_ffn_w2", "wr": "L0_ffn_wr"}


def kernel(**inputs):
    import numpy as _np
    import concourse.bacc as _bacc
    from concourse import mybir as _mybir
    from concourse.bass_utils import run_bass_kernel_spmd as _run

    nc = _bacc.Bacc("TRN2", target_bir_lowering=False, num_devices=1)
    arrays, aps = {}, {}
    for short, name in _INS.items():
        v = _np.ascontiguousarray(inputs[name])
        arrays[f"in_{short}_dram"] = v
        aps[short] = nc.dram_tensor(f"in_{short}_dram", v.shape, _mybir.dt.from_np(v.dtype), kind="ExternalInput").ap()
    out = nc.dram_tensor("out_0_dram", (NB, S, T), _mybir.dt.from_np(_np.dtype("float32")), kind="ExternalOutput").ap()
    build(nc, aps, out)
    r = _run(nc, [arrays], core_ids=[0])
    return r.results[0]["out_0_dram"]
```

```python
from contextlib import ExitStack

import concourse.bass as bass
from concourse import mybir

ALU = mybir.AluOpType
ACT = mybir.ActivationFunctionType
AX = mybir.AxisListType
F32 = mybir.dt.float32
F16 = mybir.dt.float16
BF16 = mybir.dt.bfloat16
I32 = mybir.dt.int32
U32 = mybir.dt.uint32
RMAX = bass.bass_isa.ReduceOp.max

P = 128
NB = 16
S = 256
T = 1024
TC = 512
HD = 32
NE = 8
CH = S // P
TT = T // P
CT = TC // P
PAIRS = NB // 2
TOK = 2 * S
FT = T // P
KT = TOK // P
GROUPS = FT + 2 * KT
STAGES = 15
EPS = 1e-5
SCORE = 1.0 / float(S // 8 ** 0.5)
XS = 1024.0
WS = 1024.0
TS = 64.0
MS = 8.0
SMALL = 16 * 15
W1_TR = range(3, 7)
ROUTER_FIRST = (7, 8, 9)
ROUTER = (6, 7, 8)
H1S = 2.0 ** -16
H2S = 2.0 ** -16



def build(nc, a, out):
    ctx = ExitStack()

    def sb(name, shape, dt=F32):
        return ctx.enter_context(nc.sbuf_tensor(name, shape, dt))

    def sem(name):
        return ctx.enter_context(nc.semaphore(name))

    def need(eng, s, count):
        if isinstance(count, int) and count <= 0:
            return
        eng.wait_ge(s, count)

    def w3_banks(g, middle=False):
        if middle:
            return range(18, 20) if g == 0 else ()
        return range(16, 18) if g == 0 else range(18 + 2 * g, 20 + 2 * g) if g < FT - 1 else ()

    def first_pair(j):
        return isinstance(j, int) and j == 0

    def token_stages(j):
        return (12, 14) if first_pair(j) else (13, 14)

    with ctx:
        w1b = sb("w1b", [P, FT, 2, T], F16)
        w3b = sb("w3b", [P, FT, 2, T], F16)
        w1_hi, w1_lo, w3_hi, w3_lo = w1b[:, :, 0], w1b[:, :, 1], w3b[:, :, 0], w3b[:, :, 1]
        w1f, w3f = (w[:, :, :, :].rearrange("p k a t -> p (k a t)").bitcast(F32) for w in (w1b, w3b))
        w1n, w3n = (w.rearrange("p (k f c) -> p k f c", k=FT, f=FT) for w in (w1f, w3f))
        w2t = w1f.rearrange("p (t n) -> p t n", t=FT)
        xt_hi = sb("xt_hi", [P, TT, TOK], F16)
        xt_lo = sb("xt_lo", [P, TT, TOK], F16)
        h1_hi = sb("h1_hi", [P, FT, TOK], F16)
        h1_lo = sb("h1_lo", [P, FT, TOK], F16)
        xbuf = sb("xbuf", [P, 2, 2, CH, T], F32)
        xa = [xbuf[:, 0, b] for b in range(2)]
        xs = [xbuf[:, 1, b] for b in range(2)]
        w2st = xbuf[:, :, :, :, :].rearrange("p a b c t -> p (a b c) t")
        x_hi = sb("x_hi", [P, 2, CH, T], F16)
        x_lo = sb("x_lo", [P, 2, CH, T], F16)
        ya = sb("ya", [P, CH, TC])
        y_hi = [x_hi[:, b, 0, :].rearrange("p (c t) -> p c t", c=CH) for b in range(2)]
        y_lo = [x_hi[:, b, 1, :].rearrange("p (c t) -> p c t", c=CH) for b in range(2)]
        ub = sb("ub", [P, 2, 2048])
        qk = [ub[:, b, :].rearrange("p (t n) -> p t n", t=CT) for b in range(2)]
        u = [ub[:, b, :].rearrange("p (t n) -> p t n", t=TT) for b in range(2)]
        mrow = sb("mrow", [P, T])
        mtmp = sb("mtmp", [P, TC])
        act_t = sb("act_t", [P, 2, TOK])
        bv_b = act_t[:, 1, S:2 * S].rearrange("p (c n) -> p c n", c=CH)
        h2_hi = sb("h2_hi", [P, 3, TOK], F16)
        h2_lo = sb("h2_lo", [P, 3, TOK], F16)
        sblk = sb("sblk", [P, 2, CH, P])
        t1_hi = sb("t1_hi", [P, CH, S], F16)
        t1_lo = sb("t1_lo", [P, CH, S], F16)
        m_hi = sb("m_hi", [P, 2, CH, S], F16)
        m_lo = sb("m_lo", [P, 2, CH, S], F16)
        cb = sb("cb", [P, 2, S])
        bo_b = sb("bo_b", [P, S])
        qkb_b = sb("qkb_b", [P, 2 * S])
        wqk_hi = sb("wqk_hi", [P, CH, 2 * S], F16)
        wqk_lo = sb("wqk_lo", [P, CH, 2 * S], F16)
        wo_t = sb("wo_t", [P, CH, S])
        wv_hi = sb("wv_hi", [P, CH, S], F16)
        wv_lo = sb("wv_lo", [P, CH, S], F16)
        bv_hi = sb("bv_hi", [P, CH, P], F16)
        bv_lo = sb("bv_lo", [P, CH, P], F16)
        wr_t = sb("wr_t", [P, FT, 2 * NE], F16)
        acc = sb("acc", [P, FT, 2 * NE])
        ident = sb("ident", [P, P])
        mtab = sb("mtab", [P, PAIRS, 56])
        mcur = sb("mcur", [P, 56])
        m1c = mcur[:, 0:16].rearrange("p (b t) -> p b t", b=2)
        m2c = mcur[:, 16:32].rearrange("p (b t) -> p b t", b=2)
        m2s = mcur[:, 32:48].rearrange("p (b t) -> p b t", b=2)
        mcc = mcur[:, 48:56].rearrange("p (b t) -> p b t", b=2)
        minus = sb("minus", [P, 8])
        nhalf = sb("nhalf", [P, 8])
        bst = sb("bst", [P, 8, 6])
        bst2 = sb("bst2", [P, 8, 6])
        mv = sb("mv", [P, 2, 2])
        mv2 = sb("mv2", [P, 2, 2])
        mvc = sb("mvc", [P, 8, 2])
        co = sb("co", [P, 4, 2])
        co2 = sb("co2", [P, 4, 2])
        coc = sb("coc", [P, 5, 8])
        dg = sb("dg", [P, CH, HD])
        dr = sb("dr", [P, 3, CH])
        gcol = sb("gcol", [P, 2, CH])
        tg = sb("tg", [P, 2])
        wsum = sb("wsum", [P, 2, FT])
        sc = sb("sc", [P, 4, 4])
        ysc = sb("ysc", [P, 2, 4])
        fs = sb("fs", [P, 5])
        lg = sb("lg", [P, KT, 2 * NE])
        lgs = sb("lgs", [P, KT, NE])
        top = sb("top", [P, KT, 8])
        topi = sb("topi", [P, KT, 8], U32)
        topf = sb("topf", [P, KT, 2])
        spare = sb("spare", [P, 1])
        pspare = sb("pspare", [P, 1])
        gd = sb("gd", [P, 4, KT])
        iot = sb("iot", [P, NE])
        e1t = sb("e1t", [P, KT, NE])
        e2t = sb("e2t", [P, KT, NE])
        gts = sb("gts", [P, KT, 2 * NE], F16)
        acs = qkb_b[:, 0:FT * NE].rearrange("p (f n) -> p f n", f=FT)
        wrs = x_hi[0:NE, 0].rearrange("p c t -> p (c t)").bitcast(F32)
        out8 = x_lo[0:NE, 0].rearrange("p c t -> p (c t)").bitcast(F32)

        bank = [ctx.enter_context(nc.psum_tensor(f"bank{n}", [P, 512], F32)) for n in range(8)]
        att = bank[0:4]
        fbk = bank[4:6]
        rbk, abk = bank[6], bank[7]
        wbk = bank[4:8]

        x_in = [sem(f"x_in{b}") for b in range(2)]
        out_done = [sem(f"out_done{b}") for b in range(2)]
        names = """y_in mrow_in w1a_in w1b_in w3a_in w3b_in small_in
            ident_set s_zero sc_zero w_rows w_max w_all w_clamp w_bits w_scale w_tr w_hi w_lo wr_tr wr_hi wr_lo
            ws_stat ws_mv ws_var ws_rstd ws_coef ws_norm ws_tr ws_copy ws_lo
            mask_tr mask_copy mask_sq tg_set gcol_set bias_set fs_part fs_set
            mcur_set ln1_stat ln1_mv ln1_var ln1_rstd ln1_coef xs_ready xhi_ready xlo_ready mtmp_step xpre_ready
            y_max y_all y_clamp y_bits y_scale y_hi_set y_split
            qk_mm qk_evac q_ready sc_mm sm_copy sm_max sm_sub sm_exp sm_sum sm_rec s_ready
            wv_hi_set wv_lo_set bv_hi_set bv_lo_set cb_scale t1_mm t1_high t1_evac mt_mm mt_hi mt_lo cb_mm cb_evac
            ub_part ub_ready e_mm e_xt u_ready u_stat cn_mv cn_var cn_rstd cn_mask cn_coef v_ready
            f_mm x2_ready ln2_stat ln2_mv ln2_var ln2_rstd ln2_coef xs2_ready g_mm xt_hi_set xt_lo_set
            z_mm th_ready z_used h_hi h_lo acc_mm acc_ready
            rt_mm rt_copy rt_sum rt_max rt_idx rt_idx2 rt_gap rt_exp rt_den rt_g1 rt_g2 rt_eq rt_sel rt_gate
            gates_hi gates_ready
            w2_in w2_tr w2_copy acs_set fin_mm fin_ready row_in fin_out""".split()
        sm = {n: sem(n) for n in names}

        xd = a["x"].rearrange("q (h p) t -> q p h t", p=P)
        yd = a["ctx"].rearrange("q (h p) t -> q p h t", p=P)
        od = out.rearrange("q (h p) t -> q p h t", p=P)
        wn = ub[:, 0, :].rearrange("p (w n) -> p w n", w=8)
        ws = ub[:, 1, :].rearrange("p (w n) -> p w n", w=8)
        msk = act_t[:, 0, 0:P]
        mskc = act_t[0:NB * CT, 0, P:2 * P]
        vrow = act_t[0:6, 0, 2 * P:3 * P]
        vcol = act_t[:, 1, 0:6]
        graw = act_t[:, 1, 8:10]

        smalls = [(wn[:, 2 * n:2 * n + 2, :], a[w].rearrange("(c p) n -> p c n", p=P))
                  for n, w in enumerate(("wq", "wk", "wv", "wo"))]
        smalls += [(wrs, a["wr"]), (msk, a["mask"].rearrange("q o (t p) -> (q o t) p", p=P)),
                   (mskc, a["mask_cond"].rearrange("q o (t p) -> (q o t) p", p=P)),
                   (qkb_b[:, 0:S], a["bq"].partition_broadcast(P)), (qkb_b[:, S:2 * S], a["bk"].partition_broadcast(P)),
                   (bo_b[:, :], a["bo"].partition_broadcast(P)),
                   (vrow[0:2, :], a["bv"].rearrange("(c p) -> c p", p=P)),
                   (vrow[2:4, :], a["gamma"].rearrange("(c p) -> c p", p=P)),
                   (vrow[4:6, :], a["beta"].rearrange("(c p) -> c p", p=P)),
                   (graw[:, 0:1], a["g_xattn"].partition_broadcast(P)),
                   (graw[:, 1:2], a["g_ffn"].partition_broadcast(P))]
        assert SMALL == 16 * len(smalls)

        block = ctx.enter_context(nc.Block())

        @block.sync
        def _(sp):
            def load_x(j):
                for b in range(2):
                    need(sp, out_done[b], 16 * j)
                    need(sp, sm["xs2_ready"], 2 * j + b - 1)
                    sp.dma_start(xa[b], xd[2 * j + b]).then_inc(x_in[b], 16)

            def load_y(q):
                need(sp, sm["y_split"], q)
                sp.dma_start(ya[:, :, :], yd[q]).then_inc(sm["y_in"], 16)

            def load_mask(q):
                need(sp, sm["xpre_ready"], q)
                sp.dma_start(mrow[:, :], a["mask"][q, 0, :].partition_broadcast(P)).then_inc(sm["mrow_in"], 16)

            def store(j):
                for b in range(2):
                    q = 2 * j + b
                    need(sp, sm["x2_ready"], 4 * q + 4)
                    sp.dma_start(od[q], xa[b]).then_inc(out_done[b], 16)

            def pair(j, last=False):
                load_x(j)
                for q in (2 * j + 1,) if last else (2 * j + 1, 2 * j + 2):
                    load_y(q)
                    load_mask(q)
                store(j)

            load_x(0)
            for dst, src in smalls[8:]:
                sp.dma_start(dst, src).then_inc(sm["small_in"], 16)
            load_y(0)
            load_mask(0)
            sp.wait_ge(sm["small_in"], SMALL)
            for w, dst in (("w1", w1n), ("w3", w3n)):
                for k in range(FT):
                    sp.dma_start(dst[:, k], a[w].rearrange("(f p) (k c) -> k p f c", p=P, c=P)[k])\
                        .then_inc(sm[w + "ab"[k // 4] + "_in"], 16)
            for q in (1, 2):
                load_y(q)
                load_mask(q)
            store(0)
            with sp.Fori(0, PAIRS - 2) as i:
                pair(i + 1)
            pair(PAIRS - 1, last=True)
            for b in range(2):
                sp.wait_ge(out_done[b], 16 * PAIRS)
            sp.wait_ge(sm["g_mm"], 4 * NB)
            sp.dma_start(w2st, a["w2"].rearrange("(f p) d -> p f d", p=P)).then_inc(sm["w2_in"], 16)
            sp.dma_start(wrs, out[0, 0:NE, :]).then_inc(sm["row_in"], 16)
            sp.wait_ge(sm["fin_ready"], 2)
            sp.dma_start(out[0, 0:NE, :], out8).then_inc(sm["fin_out"], 16)
            sp.wait_ge(sm["fin_out"], 16)

        @block.gpsimd
        def _(pool):
            pool.memset(ident[:, :], 0.0)
            pool.memset(nhalf[:, :], -0.5)
            pool.memset(minus[:, :], -1.0)
            pool.memset(sc[:, :, :], 0.0).then_inc(sm["sc_zero"], 1)
            pool.memset(sblk[:, :, :, :], 0.0)
            pool.memset(acc[:, :, :], 0.0).then_inc(sm["acc_ready"], 1)
            pool.memset(bv_b[:, :, :], 1.0)
            pool.iota(iot[:, :], pattern=[[1, NE]], base=0, channel_multiplier=0,
                      allow_small_or_imprecise_dtypes=True).then_inc(sm["s_zero"], 1)
            pool.wait_ge(sm["s_zero"], 1)
            pool.affine_select(out=ident[:, :], in_=ident[:, :], compare_op=ALU.not_equal, fill=1.0,
                               base=0, pattern=[[-1, P]], channel_multiplier=1).then_inc(sm["ident_set"], 1)

            def coefs(q, mvt, cot, n, eps, scale, what, used, mask=None):
                s_mv, s_var, s_rstd, s_coef = (sm[what + x] for x in ("_mv", "_var", "_rstd", "_coef"))
                pool.wait_ge(s_mv, q + 1)
                if used is not None:
                    need(pool, *used)
                pool.tensor_tensor(cot[:, 1, 0:n], mvt[:, 0:n, 0], minus[:, 0:n], ALU.mult)
                pool.tensor_scalar(cot[:, 0, 0:n], mvt[:, 0:n, 1], eps, scale ** -2, ALU.add, ALU.mult)\
                    .then_inc(s_var, 1)
                pool.wait_ge(s_var, q + 1)
                if mask is None:
                    pool.tensor_tensor(cot[:, 2, 0:n], cot[:, 0, 0:n], nhalf[:, 0:n], ALU.pow).then_inc(s_rstd, 1)
                else:
                    pool.tensor_tensor(cot[:, 4, 0:n], cot[:, 0, 0:n], nhalf[:, 0:n], ALU.pow)\
                        .then_inc(sm["cn_mask"], 1)
                    pool.wait_ge(sm["cn_mask"], q + 1)
                    pool.tensor_tensor(cot[:, 2, 0:n], cot[:, 4, 0:n], mask, ALU.mult).then_inc(s_rstd, 1)
                pool.wait_ge(s_rstd, q + 1)
                pool.tensor_tensor(cot[:, 3, 0:n], cot[:, 1, 0:n], cot[:, 2, 0:n], ALU.mult).then_inc(s_coef, 1)

            def largest(n, k):
                pool.wait_ge(sm["w_max"], n + 1)
                pool.partition_all_reduce(sc[:, k, 1:2], sc[:, k, 0:1], P, RMAX).then_inc(sm["w_all"], 1)


            def y_largest(q, b):
                pool.wait_ge(sm["y_max"], q + 1)
                pool.tensor_tensor(pspare[:, :], minus[:, 0:1], minus[:, 0:1], ALU.mult)
                pool.partition_all_reduce(ysc[:, b, 1:2], ysc[:, b, 0:1], P, RMAX).then_inc(sm["y_all"], 1)

            def ln1(q):
                coefs(q, mv, co, CH, EPS, XS, "ln1", (sm["xs_ready"], q))

            def x_low(q, b):
                pool.wait_ge(sm["xhi_ready"], q + 1)
                pool.tensor_tensor(x_lo[:, b], xs[b], x_hi[:, b], ALU.subtract).then_inc(sm["xlo_ready"], 1)

            def add_beta(q, b, c):
                for n in (2 * c, 2 * c + 1):
                    h = slice(TC * (n % 2), TC * (n % 2) + TC)
                    if n == 0:
                        pool.wait_ge(sm["mrow_in"], 16 * (q + 1))
                        pool.wait_ge(sm["xs_ready"], q + 1)
                        pool.wait_ge(sm["gcol_set"], 1)
                        need(pool, sm["xpre_ready"], q)
                    else:
                        pool.wait_ge(sm["mtmp_step"], 7 * q + 2 * n)
                    pool.tensor_tensor(mtmp[:, :], mrow[:, h], gcol[:, 1, c:c + 1].broadcast_to([P, TC]), ALU.mult)\
                        .then_inc(sm["mtmp_step"], 1)
                    pool.wait_ge(sm["mtmp_step"], 7 * q + 2 * n + 1)
                    pool.tensor_tensor(xa[b][:, c, h], xa[b][:, c, h], mtmp[:, :], ALU.add)\
                        .then_inc(sm["mtmp_step" if n < 3 else "xpre_ready"], 1)

            def attention(j, s):
                if s in (0, 1):
                    y_largest(2 * j + s, s)
                if s == 1 and first_pair(j):
                    largest(2, 0)
                if s in (3, 4) and not first_pair(j):
                    ln1(2 * j + s - 3)
                if s in (2, 3):
                    b = s - 2
                    pool.wait_ge(sm["sm_copy"], 2 * j + b + 1)
                    pool.tensor_tensor(u[b], bo_b[:, :].unsqueeze(1).broadcast_to([P, TT, S]),
                                       m1c[:, b, :].unsqueeze(2).broadcast_to([P, TT, S]), ALU.mult)\
                        .then_inc(sm["ub_part"], 1)
                if s in (5, 6):
                    x_low(2 * j + s - 5, s - 5)
                if s in (1, 2) and first_pair(j):
                    add_beta(s - 1, s - 1, 0)
                    add_beta(s - 1, s - 1, 1)
                if s in (7, 8):
                    b, q = s - 7, 2 * j + s - 7
                    if s == 7 and not first_pair(j):
                        add_beta(q, b, 0)
                    coefs(q, mvc, coc, TT, EPS * XS * XS, 1.0, "cn", (sm["v_ready"], TT * q), m1c[:, b, :])
                    if s == 8 and not first_pair(j):
                        add_beta(q, b, 0)
                    if not first_pair(j):
                        add_beta(q, b, 1)
                if s in (10, 11):
                    b, q = s - 10, 2 * j + s - 10
                    coefs(q, mv2, co2, CH, EPS, XS, "ln2", (sm["xs2_ready"], q))

            ln1(0)
            ln1(1)
            coefs(0, mvc, coc, 8, EPS, 1.0, "ws", None)
            largest(0, 2)
            largest(1, 3)
            for s in range(STAGES):
                attention(0, s)
            largest(3, 1)
            with pool.Fori(0, PAIRS - 1) as i:
                for s in range(STAGES):
                    attention(i + 1, s)

        @block.tensor
        def _(pe):
            def prepare():
                pe.wait_ge(sm["ident_set"], 1)
                pe.wait_ge(sm["small_in"], SMALL)
                pe.transpose(fbk[0][:, 0:P], msk, ident[:, :])
                pe.transpose(fbk[0][:, P:P + NB * CT], mskc, ident[0:NB * CT, 0:NB * CT])
                pe.transpose(fbk[0][:, 2 * P:2 * P + 6], vrow, ident[0:6, 0:6]).then_inc(sm["mask_tr"], 1)
                for d in range(FT):
                    last = pe.transpose(fbk[1][:, NE * d:NE * d + NE], wrs[:, P * d:P * d + P], ident[0:NE, 0:NE])
                last.then_inc(sm["wr_tr"], 1)
                pe.wait_ge(sm["ws_norm"], 8)
                for n in range(3):
                    for r in range(4):
                        w, o, c = (r // 2, r % 2, n) if n < 2 else (3, r % 2, r // 2)
                        last = pe.transpose(att[n][:, P * r:P * r + P], ws[:, 2 * w + o, P * c:P * c + P], ident[:, :])
                    last.then_inc(sm["ws_tr"], 1)
                pe.wait_ge(sm["ws_copy"], 3)
                pe.wait_ge(sm["ws_lo"], 2)
                pe.wait_ge(sm["wv_lo_set"], 1)
                pe.wait_ge(sm["bv_lo_set"], 1)

            def weight(i):
                src, n = (w1n, w3n)[i // 16], i % 16
                if i == 0:
                    pe.wait_ge(sm["mask_copy"], 1)
                    pe.wait_ge(sm["wr_lo"], 1)
                if n == 0:
                    for half in "ab":
                        pe.wait_ge(sm[f"w{1 + 2 * (i // 16)}{half}_in"], 64)
                need(pe, sm["w_lo"], i - 3 if i < 16 else i - 1)
                bk = wbk[i % 4] if i < 16 else wbk[2 + i % 2]
                for r in range(4):
                    last = pe.transpose(bk[:, P * r:P * r + P], src[:, n // 2, 4 * (n % 2) + r, :], ident[:, :])
                last.then_inc(sm["w_tr"], 1)

            def project(q, b, t):
                if t == 0:
                    pe.wait_ge(sm["y_split"], q + 1)
                if b == 0:
                    need(pe, sm["xt_lo_set"], 4 * q - 3 + t)
                elif t == 2:
                    pe.wait_ge(sm["sm_copy"], q)
                n = 0
                for c in range(CH):
                    for left, right in ((y_hi, wqk_hi), (y_hi, wqk_lo), (y_lo, wqk_hi)):
                        mm = pe.matmul(att[t][:, :], left[b][:, c, P * t:P * t + P], right[:, c, :],
                                       start=n == 0, stop=n == 5)
                        n += 1
                mm.then_inc(sm["qk_mm"], 1)

            def scores(q, b):
                pe.wait_ge(sm["q_ready"], CT * (q + 1))
                for g in range(CH):
                    for t in range(CT):
                        mm = pe.matmul(att[2][:, P * g:P * g + P], qk[b][:, t, P * g:P * g + P],
                                       qk[b][:, t, S + P * g:S + P * g + P], start=t == 0, stop=t == CT - 1)
                mm.then_inc(sm["sc_mm"], 1)

            def out_times_scores(q, b):
                pe.wait_ge(sm["s_ready"], q + 1)
                if b == 1:
                    pe.wait_ge(sm["cb_evac"], q)
                for g in range(CH):
                    mm = pe.matmul(att[3][:, S * g:S * g + S], sblk[:, b, g, :], wo_t[:, g, :], start=True, stop=True)
                mm.then_inc(sm["t1_mm"], 1)

            def times_value(q, b):
                pe.wait_ge(sm["t1_evac"], q + 1)
                need(pe, *((sm["sm_copy"], q + 2) if b == 0 else (sm["mt_lo"], q)))
                parts = ((wv_hi, t1_hi), (wv_hi, t1_lo), (wv_lo, t1_hi))
                for c in range(CH):
                    for g in range(CH):
                        for n, (left, right) in enumerate(parts):
                            mm = pe.matmul(att[2][:, S * c:S * c + S], left[:, g, P * c:P * c + P], right[:, g, :],
                                           start=g == 0 and n == 0, stop=g == CH - 1 and n == 2)
                mm.then_inc(sm["mt_mm"], 1)
                for g in range(CH):
                    for n, (left, right) in enumerate(((bv_hi, t1_hi), (bv_hi, t1_lo), (bv_lo, t1_hi))):
                        mm = pe.matmul(att[3][:, 0:S], left[:, g, :], right[:, g, :],
                                       start=g == 0 and n == 0, stop=g == CH - 1 and n == 2)
                mm.then_inc(sm["cb_mm"], 1)

            def long_product(q, b, t):
                if t == 0:
                    pe.wait_ge(sm["xlo_ready"], q + 1)
                    pe.wait_ge(sm["mt_lo"], q + 1)
                if t >= 4 or b == 1:
                    need(pe, sm["u_ready"], TT * q + t - 3)
                elif t >= 2:
                    pe.wait_ge(sm[("mt_lo", "cb_evac")[t - 2]], q + 2)
                bk = att[t % 4]
                for c in range(CH):
                    pe.transpose(bk[:, P * c:P * c + P], xs[b][:, c, P * t:P * t + P], ident[:, :])
                n = 0
                for c in range(CH):
                    for left, right in ((x_hi, m_hi), (x_hi, m_lo), (x_lo, m_hi)):
                        mm = pe.matmul(bk[:, S:2 * S], left[:, b, c, P * t:P * t + P], right[:, b, c, :],
                                       start=n == 0, stop=n == 5)
                        n += 1
                mm.then_inc(sm["e_mm"], 1)

            def attention_back(q, b, n):
                pe.wait_ge(sm["v_ready"], TT * q + 4 * (n % 2) + 4)
                if b == 1:
                    need(pe, sm["x2_ready"], 4 * q + n - 3)
                else:
                    need(pe, sm["u_ready"], TT * (q + 1) + 5 + n)
                for r in range(4):
                    mm = pe.transpose(att[n][:, P * r:P * r + P],
                                      u[b][:, 4 * (n % 2) + r, P * (n // 2):P * (n // 2) + P], ident[:, :])
                mm.then_inc(sm["f_mm"], 1)

            def tokens_transposed(q, b, n):
                if n == 0:
                    pe.wait_ge(sm["xs2_ready"], q + 1)
                if b == 1:
                    need(pe, sm["xt_lo_set"], 4 * q + n - 3)
                else:
                    need(pe, sm["x2_ready"], 4 * (q + 1) + n + 1)
                for r in range(4):
                    t, c = 2 * n + r // 2, r % 2
                    mm = pe.transpose(att[n][:, P * r:P * r + P], xs[b][:, c, P * t:P * t + P], ident[:, :])
                mm.then_inc(sm["g_mm"], 1)

            def attention(j, s, d):
                b = s % 2
                if s == 0 and d in (4, 5, 6, 7):
                    project(2 * j, 0, (4, 5, 6, 7).index(d))
                elif s == 2 and d in (3, 4, 6, 7):
                    project(2 * j + 1, 1, (3, 4, 6, 7).index(d))
                elif s in (1, 3) and d == 2:
                    scores(2 * j + s // 2, s // 2)
                elif s in (3, 4) and d == 4:
                    out_times_scores(2 * j + s - 3, s - 3)
                elif (s, d) in ((4, 0), (5, 2)):
                    times_value(2 * j + s - 4, s - 4)
                elif s in (7, 8):
                    b = s - 7
                    long_product(2 * j + b, b, d)
                elif s in (10, 11) and d % 2 == 0:
                    attention_back(2 * j + b, b, d // 2)
                elif s in token_stages(j) and d % 2 == 0:
                    b = token_stages(j).index(s)
                    tokens_transposed(2 * j + b, b, d // 2)

            def ffn(j, g, d):
                if g == GROUPS:
                    j, g = j + 1, 0
                bk = fbk[g % 2]
                if d == 0 and g == 0:
                    need(pe, sm["z_used"], GROUPS * j - 1)
                if d == 0 and g >= 1:
                    need(pe, sm["z_used"], GROUPS * j + g - 1)
                if g < FT:
                    if g == 0 and d == 0:
                        pe.wait_ge(sm["xt_lo_set"], 8 * (j + 1))
                    f = slice(P * g, P * g + P)
                    parts = ((w1_hi[:, d, f], xt_hi[:, d, :]), (w1_hi[:, d, f], xt_lo[:, d, :]),
                             (w1_lo[:, d, f], xt_hi[:, d, :]))
                else:
                    if g == FT:
                        pe.wait_ge(sm["h_lo"], GROUPS * j + d + 1)
                    k, f = (g - FT) // 2, slice(TOK * (g % 2), TOK * (g % 2) + TOK)
                    tok = slice(P * k, P * k + P)
                    parts = ((h1_hi[:, d, tok], w3_hi[:, d, f]), (h1_hi[:, d, tok], w3_lo[:, d, f]),
                             (h1_lo[:, d, tok], w3_hi[:, d, f]))
                for n, (left, right) in enumerate(parts):
                    mm = pe.matmul(bk[:, :], left, right, start=d == 0 and n == 0, stop=d == FT - 1 and n == 2)
                if d == FT - 1:
                    mm.then_inc(sm["z_mm"], 1)

            def router(j):
                for k in range(KT):
                    for d in range(FT):
                        for n, x in enumerate((xt_hi, xt_lo)):
                            mm = pe.matmul(rbk[:, 16 * k:16 * k + 16], x[:, d, P * k:P * k + P], wr_t[:, d, :],
                                           start=d == 0 and n == 0, stop=d == FT - 1 and n == 1)
                mm.then_inc(sm["rt_mm"], 1)

            def gated_sum(j, g):
                pe.wait_ge(sm["h_lo"], GROUPS * j + g + 1)
                if g == FT:
                    pe.wait_ge(sm["gates_ready"], j + 1)
                    pe.wait_ge(sm["acc_ready"], j + 1)
                k = (g - FT) // 2
                for m in range(4):
                    blk = 4 * (g % 2) + m
                    for n, h in enumerate((h2_hi, h2_lo)):
                        mm = pe.matmul(abk[:, 16 * blk:16 * blk + 16], h[:, g % 3, P * m:P * m + P], gts[:, k, :],
                                       start=g == FT and m == 0 and n == 0, stop=g == GROUPS - 1 and m == 3 and n == 1,
                                       skip_group_check=True)
                mm.then_inc(sm["acc_mm"], 1)

            def value_out(n):
                k, h = n // 2, n % 2
                if n == 0:
                    pe.wait_ge(sm["w2_in"], 16)
                need(pe, sm["w2_copy"], n - 3)
                for r in range(4):
                    mm = pe.transpose(att[n % 4][:, P * r:P * r + P], w2st[:, 4 * h + r, P * k:P * k + P], ident[:, :])
                mm.then_inc(sm["w2_tr"], 1)

            def group(j, g, ja=None, w3=False):
                for d in range(FT):
                    if w3 and d in (0, FT // 2):
                        for i in w3_banks(g, d > 0):
                            weight(i)
                    if ja is not None:
                        attention(ja, g - 1, d)
                    ffn(j, g, d)
                if g == (ROUTER_FIRST if w3 else ROUTER)[0]:
                    if w3:
                        pe.wait_ge(sm["w_lo"], 32)
                    router(j)
                if g >= FT + 2:
                    gated_sum(j, g - 2)
                if g == 1 and not first_pair(j):
                    gated_sum(j - 1, GROUPS - 1)

            def result(ks):
                for h in range(2):
                    for k in ks:
                        mm = pe.matmul(att[h][0:NE, :], acs[:, k, :], w2t[:, k, 512 * h:512 * h + 512],
                                       start=k == 0, stop=k == FT - 1)
                    if k == FT - 1:
                        mm.then_inc(sm["fin_mm"], 1)

            prepare()
            for s in range(STAGES):
                if s in W1_TR:
                    for i in range(4):
                        weight(4 * (s - W1_TR[0]) + i)
                for d in range(FT):
                    attention(0, s, d)
            pe.wait_ge(sm["w_lo"], 16)
            group(0, 0, w3=True)
            for g in range(1, GROUPS + 1):
                group(0, g, 1, w3=True)
            with pe.Fori(0, PAIRS - 2) as i:
                for g in range(1, GROUPS + 1):
                    group(i + 1, g, i + 2)
            for g in range(1, GROUPS):
                group(PAIRS - 1, g)
                if FT - 1 <= g < GROUPS - 1:
                    value_out(2 * (g - FT + 1))
                    value_out(2 * (g - FT + 1) + 1)
            gated_sum(PAIRS - 1, GROUPS - 2)
            pe.wait_ge(sm["w2_copy"], 2 * FT)
            pe.wait_ge(sm["acs_set"], 1)
            result(range(0, FT // 2))
            gated_sum(PAIRS - 1, GROUPS - 1)
            pe.wait_ge(sm["acs_set"], 2)
            result(range(FT // 2, FT))

        @block.scalar
        def _(act):
            def normed(q, b, c_, s_coef, s_done):
                act.wait_ge(s_coef, q + 1)
                for c in range(CH):
                    ins = act.activation(xs[b][:, c, :], xa[b][:, c, :], ACT.Identity,
                                         bias=c_[:, 3, c:c + 1], scale=c_[:, 2, c:c + 1])
                ins.then_inc(s_done, 1)

            for dst, src in smalls[:8]:
                act.dma_start(dst, src).then_inc(sm["small_in"], 16)
            for b in range(2):
                normed(b, b, co, sm["ln1_coef"], sm["xs_ready"])
            act.wait_ge(sm["small_in"], SMALL)
            act.activation(tg[:, :], graw, ACT.Tanh).then_inc(sm["tg_set"], 1)
            act.wait_ge(sm["ws_coef"], 1)
            for n in range(8):
                act.activation(ws[:, n, :], wn[:, n, :], ACT.Identity, bias=coc[:, 3, n:n + 1], scale=coc[:, 2, n:n + 1])\
                    .then_inc(sm["ws_norm"], 1)
            for n in range(3):
                act.wait_ge(sm["ws_tr"], n + 1)
                if n < 2:
                    act.activation(wqk_hi[:, n, :], att[n][:, :], ACT.Copy, scale=WS).then_inc(sm["ws_copy"], 1)
                else:
                    act.activation(wo_t[:, :, :], att[n][:, :].rearrange("p (c n) -> p c n", c=CH), ACT.Copy)\
                        .then_inc(sm["ws_copy"], 1)
            act.wait_ge(sm["ws_norm"], 8)
            act.activation(wv_hi[:, :, :], ws[:, 4:6, :], ACT.Copy, scale=WS).then_inc(sm["wv_hi_set"], 1)
            act.wait_ge(sm["w_scale"], 2)
            act.wait_ge(sm["bias_set"], 1)
            act.activation(bv_hi[:, :, :], bv_b[:, :, :], ACT.Copy, scale=sc[:, 3, 2:3]).then_inc(sm["bv_hi_set"], 1)
            act.wait_ge(sm["w_scale"], 1)
            act.wait_ge(sm["wr_tr"], 1)
            act.activation(wr_t[:, :, 0:NE], fbk[1][:, 0:FT * NE].rearrange("p (d n) -> p d n", d=FT), ACT.Copy,
                           scale=sc[:, 2, 2:3]).then_inc(sm["wr_hi"], 1)

            def weight(i):
                dst, n, k = (w1_hi, w3_hi)[i // 16], i % 16, i // 16
                if n == 0:
                    act.wait_ge(sm["w_scale"], 3 + k)
                act.wait_ge(sm["w_tr"], 2 * (i // 2) + 2)
                bk = wbk[i % 4] if i < 16 else wbk[2 + i % 2]
                act.activation(dst[:, n // 2, 512 * (n % 2):512 * (n % 2) + 512], bk[:, :], ACT.Copy,
                               scale=sc[:, k, 2:3]).then_inc(sm["w_hi"], 1)

            def y_high(q, b):
                act.wait_ge(sm["y_scale"], q + 1)
                act.activation(y_hi[b], ya[:, :, :], ACT.Copy, scale=ysc[:, b, 2:3]).then_inc(sm["y_hi_set"], 1)

            def attention(j, s):
                if s in (0, 2):
                    b, q = s // 2, 2 * j + s // 2
                    for t in range(CT):
                        act.wait_ge(sm["qk_evac"], CT * q + t + 1)
                        act.activation(qk[b][:, t, 0:S], qk[b][:, t, 0:S], ACT.Copy, scale=mcc[:, b, t:t + 1])\
                            .then_inc(sm["q_ready"], 1)
                if s in (1, 3):
                    q = 2 * j + s // 2
                    act.wait_ge(sm["sm_sub"], q + 1)
                    act.activation(dg[:, :, :], dg[:, :, :], ACT.Exp, scale=SCORE).then_inc(sm["sm_exp"], 1)
                if s in (4, 5):
                    b, q = s - 4, 2 * j + s - 4
                    act.wait_ge(sm["mt_mm"], q + 1)
                    act.activation(m_hi[:, b], att[2][:, :].rearrange("p (c n) -> p c n", c=CH), ACT.Copy,
                                   scale=MS / (WS * TS))\
                        .then_inc(sm["mt_hi"], 1)
                    act.wait_ge(sm["cb_mm"], q + 1)
                    act.activation(cb[:, b, :], att[3][:, 0:S], ACT.Copy, scale=fs[:, 4:5]).then_inc(sm["cb_evac"], 1)
                if s in (3, 4):
                    q = 2 * j + s - 3
                    act.wait_ge(sm["t1_mm"], q + 1)
                    act.activation(t1_hi[:, :, :], att[3][:, :].rearrange("p (c n) -> p c n", c=CH), ACT.Copy,
                                   scale=TS).then_inc(sm["t1_high"], 1)
                if s in (8, 9):
                    b, q = s - 8, 2 * j + s - 8
                    act.wait_ge(sm["cn_coef"], q + 1)
                    for t in range(TT):
                        act.activation(u[b][:, t, :], u[b][:, t, :], ACT.Identity, bias=coc[:, 3, t:t + 1],
                                       scale=coc[:, 2, t:t + 1]).then_inc(sm["v_ready"], 1)
                if s in token_stages(j):
                    b = token_stages(j).index(s)
                    q = 2 * j + b
                    for n in range(4):
                        act.wait_ge(sm["g_mm"], 4 * q + n + 1)
                        act.activation(xt_hi[:, 2 * n:2 * n + 2, S * b:S * b + S],
                                       att[n][:, :].rearrange("p (t n) -> p t n", t=2), ACT.Copy)\
                            .then_inc(sm["xt_hi_set"], 1)
                if s in (11, 12):
                    normed(2 * j + s - 11, s - 11, co2, sm["ln2_coef"], sm["xs2_ready"])

            def attention_late(j, s):
                if s == 0:
                    y_high(2 * j + 1, 1)
                if s in (4, 5) and not first_pair(j):
                    normed(2 * j + s - 4, s - 4, co, sm["ln1_coef"], sm["xs_ready"])

            def ffn(j, g):
                first = g < FT
                act.wait_ge(sm["z_mm"], GROUPS * j + g + 1)
                act.activation(act_t[:, g % 2, :], fbk[g % 2][:, :], ACT.Tanh,
                               scale=fs[:, 0:1] if first else fs[:, 1:2]).then_inc(sm["th_ready"], 1)
                if g >= FT + 3:
                    act.wait_ge(sm["acc_mm"], 8 * j + g - FT - 2)
                act.wait_ge(sm["z_used"], GROUPS * j + g + 1)
                act.activation(h1_hi[:, g, :] if first else h2_hi[:, g % 3, :], act_t[:, g % 2, :], ACT.Copy,
                               scale=H1S if first else H2S).then_inc(sm["h_hi"], 1)

            def gates(j):
                act.wait_ge(sm["rt_gap"], j + 1)
                act.activation(gd[:, 1, :], gd[:, 0, :], ACT.Exp, scale=fs[:, 2:3]).then_inc(sm["rt_exp"], 1)

            def group(j, g, ja=None, w3=False):
                if w3:
                    for i in w3_banks(g):
                        weight(i)
                if ja is not None:
                    if g == 0:
                        y_high(2 * ja, 0)
                    else:
                        attention(ja, g - 1)
                if w3:
                    for i in w3_banks(g, middle=True):
                        weight(i)
                if w3 and g == FT:
                    act.wait_ge(sm["fs_set"], 2)
                ffn(j, g)
                if ja is not None:
                    attention_late(ja, g - 1)
                if g == (ROUTER_FIRST if w3 else ROUTER)[1]:
                    gates(j)

            def row_sums(k):
                for half in "ab":
                    act.wait_ge(sm[f"w{1 + 2 * k}{half}_in"], 64)
                for f in range(FT):
                    spoil = ((xt_hi, xt_lo), (h1_hi, h1_lo))[k][f // 4][:, 2 * (f % 4):2 * (f % 4) + 2, :]
                    spoil = spoil.rearrange("p a n -> p (a n)").rearrange("p (k c) -> p k c", k=FT)
                    act.activation(spoil.bitcast(BF16), (w1n, w3n)[k][:, :, f, :], ACT.Abs,
                                   accum_out=wsum[:, k, f:f + 1]).then_inc(sm["w_rows"], 1)

            y_high(0, 0)
            row_sums(0)
            for s in range(STAGES):
                if s in W1_TR:
                    for i in range(4):
                        weight(4 * (s - W1_TR[0]) + i)
                attention(0, s)
                attention_late(0, s)
                if s in (4, 6):
                    b = (s - 4) // 2
                    act.wait_ge(sm["qk_mm"], CT * (b + 1))
                    act.activation(x_hi[:, b], xs[b], ACT.Copy).then_inc(sm["xhi_ready"], 1)
                if s == 6:
                    row_sums(1)
            act.wait_ge(sm["fs_set"], 1)
            for g in range(GROUPS):
                group(0, g, 1, w3=True)
            with act.Fori(0, PAIRS - 2) as i:
                for g in range(GROUPS):
                    group(i + 1, g, i + 2)
            for g in range(GROUPS):
                group(PAIRS - 1, g)
                if FT - 1 <= g < GROUPS - 1:
                    for n in (2 * (g - FT + 1), 2 * (g - FT + 1) + 1):
                        act.wait_ge(sm["w2_tr"], n + 1)
                        at = slice(512 * (n % 2), 512 * (n % 2) + 512)
                        act.activation(w2t[:, n // 2, at], att[n % 4][:, :], ACT.Copy).then_inc(sm["w2_copy"], 1)

        @block.vector
        def _(dve):
            def carry():
                dve.memset(spare[:, :], 0.0)

            def y_largest(q, b):
                dve.wait_ge(sm["y_in"], 16 * (q + 1))
                dve.tensor_reduce(ysc[:, b, 0:1], ya[:, :, :], AX.XY, ALU.max, apply_absolute_value=True)\
                    .then_inc(sm["y_max"], 1)

            def y_scale(q, b):
                dve.wait_ge(sm["y_all"], q + 1)
                dve.tensor_scalar(ysc[:, b, 0:1], ysc[:, b, 1:2], 1e-30, None, ALU.max).then_inc(sm["y_clamp"], 1)
                dve.wait_ge(sm["y_clamp"], q + 1)
                si = ysc[:, b, :].bitcast(I32)
                dve.tensor_scalar(si[:, 0:1], si[:, 0:1], 0x7F800000, None, ALU.bitwise_and).then_inc(sm["y_bits"], 1)
                dve.wait_ge(sm["y_bits"], q + 1)
                dve.tensor_scalar(si[:, 2:3], si[:, 0:1], -1.0, float(268 << 23), ALU.mult, ALU.add)
                dve.tensor_scalar(si[:, 3:4], si[:, 0:1], -float(24 << 23), None, ALU.add).then_inc(sm["y_scale"], 1)

            def y_low(q, b):
                dve.wait_ge(sm["y_hi_set"], q + 1)
                dve.scalar_tensor_tensor(out=y_lo[b], in0=ya[:, :, :], scalar=ysc[:, b, 2:3], in1=y_hi[b],
                                         op0=ALU.mult, op1=ALU.subtract).then_inc(sm["y_split"], 1)

            def scale_of(n, k, src, parts):
                dve.tensor_reduce(sc[0:parts, k, 0:1], src, AX.X, ALU.max,
                                  apply_absolute_value=True).then_inc(sm["w_max"], 1)
                dve.wait_ge(sm["w_all"], n + 1)
                dve.tensor_scalar(sc[:, k, 0:1], sc[:, k, 1:2], 1e-30, None, ALU.max).then_inc(sm["w_clamp"], 1)
                dve.wait_ge(sm["w_clamp"], n + 1)
                si = sc[:, k, :].bitcast(I32)
                dve.tensor_scalar(si[:, 0:1], si[:, 0:1], 0x7F800000, None, ALU.bitwise_and)\
                    .then_inc(sm["w_bits"], 1)
                dve.wait_ge(sm["w_bits"], n + 1)
                dve.tensor_scalar(si[:, 2:3], si[:, 0:1], -1.0, float(268 << 23), ALU.mult, ALU.add)
                dve.tensor_scalar(si[:, 3:4], si[:, 0:1], -float(14 << 23), None, ALU.add)\
                    .then_inc(sm["w_scale"], 1)
                dve.wait_ge(sm["w_scale"], n + 1)

            def prepare():
                dve.wait_ge(sm["small_in"], SMALL)
                for n in range(8):
                    ins = dve.bn_stats(bst2[:, n, :], wn[:, n, :])
                ins.then_inc(sm["ws_stat"], 1)
                dve.wait_ge(sm["ws_stat"], 1)
                for n in range(8):
                    ins = dve.bn_aggr(mvc[:, n, :], bst2[:, n, :])
                ins.then_inc(sm["ws_mv"], 1)
                dve.wait_ge(sm["mask_tr"], 1)
                dve.tensor_copy(vcol, fbk[0][:, 2 * P:2 * P + 6])
                dve.tensor_copy(mtab[:, :, 0:16], fbk[0][:, 0:P].rearrange("p (j n) -> p j n", j=PAIRS))
                dve.tensor_copy(mtab[:, :, 48:56], fbk[0][:, P:P + 64].rearrange("p (j n) -> p j n", j=PAIRS))\
                    .then_inc(sm["mask_copy"], 1)
                dve.wait_ge(sm["mask_copy"], 1)
                dve.tensor_tensor(mtab[:, :, 16:32], mtab[:, :, 0:16], mtab[:, :, 0:16], ALU.mult)
                dve.tensor_tensor(mtab[:, :, 48:56], mtab[:, :, 48:56], mtab[:, :, 48:56], ALU.mult)\
                    .then_inc(sm["mask_sq"], 1)
                dve.wait_ge(sm["mask_sq"], 1)
                dve.tensor_scalar(mtab[:, :, 32:48], mtab[:, :, 16:32], 1.0 / MS, None, ALU.mult)\
                    .then_inc(sm["mask_sq"], 1)
                dve.wait_ge(sm["mask_sq"], 2)
                dve.wait_ge(sm["tg_set"], 1)
                dve.tensor_scalar(gcol[:, :, :], vcol[:, 2:6].rearrange("p (a c) -> p a c", a=2),
                                  tg[:, 0:1], None, ALU.mult).then_inc(sm["gcol_set"], 1)
                dve.tensor_scalar(bo_b[:, :], bo_b[:, :], XS, None, ALU.mult)
                dve.wait_ge(sm["s_zero"], 1)
                for g in range(CH):
                    ins = dve.tensor_scalar(bv_b[:, g, :], bv_b[:, g, :], vcol[:, g:g + 1], None, ALU.mult)
                ins.then_inc(sm["bias_set"], 1)
                dve.wait_ge(sm["bias_set"], 1)
                dve.wait_ge(sm["sc_zero"], 1)

                scale_of(0, 2, wrs, NE)
                scale_of(1, 3, vcol[:, 0:CH], P)
                dve.tensor_scalar(fs[:, 4:5], sc[:, 3, 3:4], XS / TS, None, ALU.mult).then_inc(sm["cb_scale"], 1)
                y_largest(0, 0)
                for n in range(2):
                    dve.wait_ge(sm["ws_copy"], n + 1)
                    dve.scalar_tensor_tensor(out=wqk_lo[:, n, :], in0=att[n][:, :], scalar=WS, in1=wqk_hi[:, n, :],
                                             op0=ALU.mult, op1=ALU.subtract).then_inc(sm["ws_lo"], 1)
                dve.wait_ge(sm["wv_hi_set"], 1)
                dve.scalar_tensor_tensor(out=wv_lo[:, :, :], in0=ws[:, 4:6, :], scalar=WS, in1=wv_hi[:, :, :],
                                         op0=ALU.mult, op1=ALU.subtract).then_inc(sm["wv_lo_set"], 1)
                dve.wait_ge(sm["bv_hi_set"], 1)
                dve.scalar_tensor_tensor(out=bv_lo[:, :, :], in0=bv_b[:, :, :], scalar=sc[:, 3, 2:3], in1=bv_hi[:, :, :],
                                         op0=ALU.mult, op1=ALU.subtract).then_inc(sm["bv_lo_set"], 1)
                y_scale(0, 0)
                dve.wait_ge(sm["wr_hi"], 1)
                dve.scalar_tensor_tensor(out=wr_t[:, :, NE:2 * NE],
                                         in0=fbk[1][:, 0:FT * NE].rearrange("p (d n) -> p d n", d=FT),
                                         scalar=sc[:, 2, 2:3], in1=wr_t[:, :, 0:NE], op0=ALU.mult, op1=ALU.subtract)\
                    .then_inc(sm["wr_lo"], 1)

            def weight_scale(k):
                dve.wait_ge(sm["w_rows"], FT * (k + 1))
                scale_of(2 + k, k, wsum[:, k, :], P)
                scales(k)

            def weight(i):
                (hi, lo), n, k = ((w1_hi, w1_lo), (w3_hi, w3_lo))[i // 16], i % 16, i // 16
                at = slice(512 * (n % 2), 512 * (n % 2) + 512)
                bk = wbk[i % 4] if i < 16 else wbk[2 + i % 2]
                dve.wait_ge(sm["w_hi"], i + 1)
                dve.scalar_tensor_tensor(out=lo[:, n // 2, at], in0=bk[:, :], scalar=sc[:, k, 2:3],
                                         in1=hi[:, n // 2, at], op0=ALU.mult, op1=ALU.subtract)\
                    .then_inc(sm["w_lo"], 1)

            def scales(k):
                if k == 0:
                    dve.tensor_scalar(fs[:, 0:1], sc[:, 0, 3:4], 0.5 / XS, None, ALU.mult)
                    dve.tensor_scalar(fs[:, 2:3], sc[:, 2, 3:4], 1.0 / XS, None, ALU.mult).then_inc(sm["fs_set"], 1)
                else:
                    dve.tensor_scalar(fs[:, 1:2], sc[:, 0, 3:4], sc[:, 1, 3:4], 1 / (4 * XS * H1S), ALU.mult, ALU.mult)\
                        .then_inc(sm["fs_part"], 1)
                    dve.wait_ge(sm["fs_part"], 1)
                    dve.tensor_scalar(fs[:, 3:4], fs[:, 1:2], tg[:, 1:2], 1 / H2S, ALU.mult, ALU.mult)\
                        .then_inc(sm["fs_set"], 1)

            def ln1(j, b):
                q = 2 * j + b
                dve.wait_ge(x_in[b], 16 * (j + 1))
                need(dve, sm[("ln2_mv", "ln1_mv")[b]], q)
                for n in range(4):
                    ins = dve.bn_stats(bst[:, n, :], xa[b][:, n // 2, TC * (n % 2):TC * (n % 2) + TC])
                ins.then_inc(sm["ln1_stat"], 1)
                dve.wait_ge(sm["ln1_stat"], q + 1)
                need(dve, sm["ln1_coef"], q)
                carry()
                for c in range(CH):
                    ins = dve.bn_aggr(mv[:, c, :], bst[:, 2 * c:2 * c + 2, :])
                ins.then_inc(sm["ln1_mv"], 1)

            def x_high(q, b):
                dve.wait_ge(sm["xs_ready"], q + 1)
                dve.tensor_copy(x_hi[:, b], xs[b]).then_inc(sm["xhi_ready"], 1)

            def m_low(q, b):
                dve.wait_ge(sm["mt_hi"], q + 1)
                dve.scalar_tensor_tensor(out=m_lo[:, b], in0=att[2][:, :].rearrange("p (c n) -> p c n", c=CH),
                                         scalar=MS / (WS * TS), in1=m_hi[:, b], op0=ALU.mult, op1=ALU.subtract).then_inc(sm["mt_lo"], 1)

            def softmax(q, b):
                dve.wait_ge(sm["sc_mm"], q + 1)
                for h in range(4):
                    r = slice(HD * h, HD * h + HD)
                    ins = dve.tensor_copy(dg[r, :, :], att[2][r, 0:2 * P].rearrange("p (g n) -> p g n", g=CH)[:, :, r])
                ins.then_inc(sm["sm_copy"], 1)
                dve.wait_ge(sm["sm_copy"], q + 1)
                dve.tensor_reduce(dr[:, 0, :], dg[:, :, :], AX.X, ALU.max).then_inc(sm["sm_max"], 1)
                dve.wait_ge(sm["sm_max"], q + 1)
                dve.tensor_tensor(dg[:, :, :], dg[:, :, :], dr[:, 0, :].unsqueeze(2).broadcast_to([P, CH, HD]),
                                  ALU.subtract).then_inc(sm["sm_sub"], 1)
                dve.wait_ge(sm["sm_exp"], q + 1)
                dve.tensor_reduce(dr[:, 1, :], dg[:, :, :], AX.X, ALU.add).then_inc(sm["sm_sum"], 1)
                dve.wait_ge(sm["sm_sum"], q + 1)
                dve.reciprocal(dr[:, 2, :], dr[:, 1, :]).then_inc(sm["sm_rec"], 1)
                dve.wait_ge(sm["sm_rec"], q + 1)
                for h in range(4):
                    r = slice(HD * h, HD * h + HD)
                    ins = dve.tensor_tensor(sblk[r, b, :, r], dg[r, :, :],
                                            dr[r, 2, :].unsqueeze(2).broadcast_to([HD, CH, HD]), ALU.mult)
                ins.then_inc(sm["s_ready"], 1)

            def bias_tiles(q, b):
                dve.wait_ge(sm["ub_part"], q + 1)
                dve.wait_ge(sm["cb_evac"], q + 1)
                for t in range(TT):
                    ins = dve.scalar_tensor_tensor(out=u[b][:, t, :], in0=cb[:, b, :], scalar=m2c[:, b, t:t + 1],
                                                   in1=u[b][:, t, :], op0=ALU.mult, op1=ALU.add)
                ins.then_inc(sm["ub_ready"], 1)

            def attention_out(q, b):
                dve.wait_ge(sm["ub_ready"], q + 1)

                def stats(t):
                    dve.wait_ge(sm["u_ready"], TT * q + t + 1)
                    dve.bn_stats(bst2[:, t, :], u[b][:, t, :]).then_inc(sm["u_stat"], 1)

                for t in range(TT):
                    bk = att[t % 4]
                    dve.wait_ge(sm["e_mm"], TT * q + t + 1)
                    dve.tensor_tensor(u[b][:, t, :], u[b][:, t, :], bk[:, 0:S], ALU.add).then_inc(sm["e_xt"], 1)
                    if t > 0:
                        stats(t - 1)
                    dve.wait_ge(sm["e_xt"], TT * q + t + 1)
                    dve.scalar_tensor_tensor(out=u[b][:, t, :], in0=bk[:, S:2 * S], scalar=m2s[:, b, t:t + 1],
                                             in1=u[b][:, t, :], op0=ALU.mult, op1=ALU.add).then_inc(sm["u_ready"], 1)
                stats(TT - 1)
                dve.wait_ge(sm["u_stat"], TT * (q + 1))
                need(dve, sm["cn_coef"], q)
                carry()
                for t in range(TT):
                    ins = dve.bn_aggr(mvc[:, t, :], bst2[:, t, :])
                ins.then_inc(sm["cn_mv"], 1)

            def residual(q, b):
                dve.wait_ge(sm["xpre_ready"], q + 1)
                dve.wait_ge(*((sm["ln1_mv"], q + 2) if b == 0 else (sm["ln2_mv"], q)))

                def stats(n):
                    dve.wait_ge(sm["x2_ready"], 4 * q + n + 1)
                    dve.bn_stats(bst[:, n, :], xa[b][:, n // 2, TC * (n % 2):TC * (n % 2) + TC])\
                        .then_inc(sm["ln2_stat"], 1)

                for n in range(4):
                    c, h = n // 2, slice(TC * (n % 2), TC * (n % 2) + TC)
                    dve.wait_ge(sm["f_mm"], 4 * q + n + 1)
                    dve.scalar_tensor_tensor(out=xa[b][:, c, h], in0=att[n][:, :], scalar=gcol[:, 0, c:c + 1],
                                             in1=xa[b][:, c, h], op0=ALU.mult, op1=ALU.add).then_inc(sm["x2_ready"], 1)
                    if n > 0:
                        stats(n - 1)
                stats(3)
                dve.wait_ge(sm["ln2_stat"], 4 * (q + 1))
                need(dve, sm["ln2_coef"], q)
                carry()
                for c in range(CH):
                    ins = dve.bn_aggr(mv2[:, c, :], bst[:, 2 * c:2 * c + 2, :])
                ins.then_inc(sm["ln2_mv"], 1)

            def masks(j):
                need(dve, sm["cn_coef"], 2 * j)
                need(dve, sm["q_ready"], 2 * CT * j)
                dve.tensor_copy(mcur[:, :], mtab[:, j, :]).then_inc(sm["mcur_set"], 1)
                dve.wait_ge(sm["mcur_set"], j + 1)

            def attention(j, s):
                if s in (0, 2):
                    b, q = s // 2, 2 * j + s // 2
                    for t in range(CT):
                        dve.wait_ge(sm["qk_mm"], CT * q + t + 1)
                        dve.scalar_tensor_tensor(out=qk[b][:, t, :], in0=att[t][:, :], scalar=ysc[:, b, 3:4],
                                                 in1=qkb_b[:, :], op0=ALU.mult, op1=ALU.add).then_inc(sm["qk_evac"], 1)
                if s in (1, 3):
                    softmax(2 * j + s // 2, s // 2)
                if s == 4:
                    m_low(2 * j, 0)
                if s in (3, 4):
                    q = 2 * j + s - 3
                    dve.wait_ge(sm["t1_high"], q + 1)
                    dve.scalar_tensor_tensor(out=t1_lo[:, :, :], in0=att[3][:, :].rearrange("p (c n) -> p c n", c=CH),
                                             scalar=TS, in1=t1_hi[:, :, :], op0=ALU.mult, op1=ALU.subtract)\
                        .then_inc(sm["t1_evac"], 1)
                if s in (3, 4) and not first_pair(j):
                    ln1(j, s - 3)
                if s in (5, 6):
                    bias_tiles(2 * j + s - 5, s - 5)
                if s in (5, 6) and not first_pair(j):
                    x_high(2 * j + s - 5, s - 5)
                if s == 5:
                    m_low(2 * j + 1, 1)
                if s in (7, 8):
                    attention_out(2 * j + s - 7, s - 7)
                if s in (10, 11):
                    residual(2 * j + s - 10, s - 10)
                if s in token_stages(j):
                    b = token_stages(j).index(s)
                    q = 2 * j + b
                    for n in range(4):
                        dve.wait_ge(sm["xt_hi_set"], 4 * q + n + 1)
                        dve.tensor_tensor(xt_lo[:, 2 * n:2 * n + 2, S * b:S * b + S],
                                          att[n][:, :].rearrange("p (t n) -> p t n", t=2),
                                          xt_hi[:, 2 * n:2 * n + 2, S * b:S * b + S], ALU.subtract)\
                            .then_inc(sm["xt_lo_set"], 1)

            def split_y(q, b):
                y_largest(q, b)
                y_scale(q, b)
                y_low(q, b)

            def ffn(j, g):
                buf, first = act_t[:, g % 2, :], g < FT
                dve.wait_ge(sm["th_ready"], GROUPS * j + g + 1)
                dve.scalar_tensor_tensor(out=buf, in0=buf, scalar=1.0, in1=fbk[g % 2][:, :], op0=ALU.add, op1=ALU.mult)\
                    .then_inc(sm["z_used"], 1)
                dve.wait_ge(sm["h_hi"], GROUPS * j + g + 1)
                hi = h1_hi[:, g, :] if first else h2_hi[:, g % 3, :]
                lo = h1_lo[:, g, :] if first else h2_lo[:, g % 3, :]
                dve.scalar_tensor_tensor(out=lo, in0=buf, scalar=H1S if first else H2S, in1=hi,
                                         op0=ALU.mult, op1=ALU.subtract).then_inc(sm["h_lo"], 1)

            def top_two(j):
                dve.wait_ge(sm["rt_mm"], j + 1)
                dve.tensor_copy(lg[:, :, :], rbk[:, 0:KT * 16].rearrange("p (k n) -> p k n", k=KT))\
                    .then_inc(sm["rt_copy"], 1)
                dve.wait_ge(sm["rt_copy"], j + 1)
                dve.tensor_tensor(lgs[:, :, :], lg[:, :, 0:NE], lg[:, :, NE:2 * NE], ALU.add).then_inc(sm["rt_sum"], 1)
                dve.wait_ge(sm["rt_sum"], j + 1)
                carry()
                for k in range(KT):
                    ins = dve.max(top[:, k, :], lgs[:, k, :])
                ins.then_inc(sm["rt_max"], 1)
                dve.wait_ge(sm["rt_max"], j + 1)
                dve.tensor_tensor(gd[:, 0, :], top[:, :, 1], top[:, :, 0], ALU.subtract).then_inc(sm["rt_gap"], 1)
                for k in range(KT):
                    ins = dve.max_index(topi[:, k, :], top[:, k, :], lgs[:, k, :])
                ins.then_inc(sm["rt_idx"], 1)
                dve.wait_ge(sm["rt_idx"], j + 1)
                dve.tensor_copy(topf[:, :, :], topi[:, :, 0:2]).then_inc(sm["rt_idx2"], 1)

            def gates(j):
                dve.wait_ge(sm["rt_exp"], j + 1)
                dve.tensor_scalar(gd[:, 0, :], gd[:, 1, :], 1.0, None, ALU.add).then_inc(sm["rt_den"], 1)
                dve.wait_ge(sm["rt_den"], j + 1)
                dve.reciprocal(gd[:, 2, :], gd[:, 0, :]).then_inc(sm["rt_g1"], 1)
                dve.wait_ge(sm["rt_idx2"], j + 1)
                for n, e in enumerate((e1t, e2t)):
                    ins = dve.tensor_tensor(e[:, :, :], iot[:, :].unsqueeze(1).broadcast_to([P, KT, NE]),
                                            topf[:, :, n].unsqueeze(2).broadcast_to([P, KT, NE]), ALU.is_equal)
                ins.then_inc(sm["rt_eq"], 1)
                dve.wait_ge(sm["rt_g1"], j + 1)
                dve.tensor_tensor(gd[:, 3, :], gd[:, 1, :], gd[:, 2, :], ALU.mult).then_inc(sm["rt_g2"], 1)
                dve.wait_ge(sm["rt_eq"], j + 1)
                dve.wait_ge(sm["rt_g2"], j + 1)
                for n, e in enumerate((e1t, e2t)):
                    ins = dve.tensor_tensor(e[:, :, :], e[:, :, :], gd[:, 2 + n, :].unsqueeze(2).broadcast_to([P, KT, NE]),
                                            ALU.mult)
                ins.then_inc(sm["rt_sel"], 1)
                dve.wait_ge(sm["rt_sel"], j + 1)
                dve.tensor_tensor(e1t[:, :, :], e1t[:, :, :], e2t[:, :, :], ALU.add).then_inc(sm["rt_gate"], 1)
                dve.wait_ge(sm["rt_gate"], j + 1)
                dve.tensor_copy(gts[:, :, 0:NE], e1t[:, :, :]).then_inc(sm["gates_hi"], 1)
                dve.wait_ge(sm["gates_hi"], j + 1)
                dve.tensor_tensor(gts[:, :, NE:2 * NE], e1t[:, :, :], gts[:, :, 0:NE], ALU.subtract)\
                    .then_inc(sm["gates_ready"], 1)

            def group(j, g, ja=None, w3=False):
                if w3:
                    for i in w3_banks(g):
                        weight(i)
                if ja is not None:
                    if g == 0:
                        split_y(2 * ja, 0)
                    else:
                        attention(ja, g - 1)
                if w3:
                    for i in w3_banks(g, middle=True):
                        weight(i)
                if g == (ROUTER_FIRST if w3 else ROUTER)[2]:
                    gates(j)
                ffn(j, g)
                if g == 1 and not first_pair(j):
                    add_sums(j - 1)
                if g == 0 and ja is not None:
                    masks(ja)
                if ja is not None and g == 1:
                    split_y(2 * ja + 1, 1)
                if g == (ROUTER_FIRST if w3 else ROUTER)[1]:
                    top_two(j)

            def add_sums(j):
                dve.wait_ge(sm["acc_mm"], 8 * (j + 1))
                dve.wait_ge(sm["acc_ready"], j + 1)
                dve.tensor_tensor(acc[:, :, :], acc[:, :, :], abk[:, 0:P].rearrange("p (k n) -> p k n", k=FT),
                                  ALU.add).then_inc(sm["acc_ready"], 1)

            def last_sums(h):
                blocks = slice(4 * h, 4 * h + 4)
                dve.wait_ge(sm["acc_mm"], 8 * PAIRS - 1 + h)
                dve.wait_ge(sm["acc_ready"], PAIRS + h)
                dve.tensor_tensor(acc[:, blocks, :], acc[:, blocks, :],
                                  abk[:, 64 * h:64 * h + 64].rearrange("p (k n) -> p k n", k=4), ALU.add)\
                    .then_inc(sm["acc_ready"], 1)
                dve.wait_ge(sm["acc_ready"], PAIRS + 1 + h)
                dve.tensor_tensor(acs[:, blocks, :], acc[:, blocks, 0:NE], acc[:, blocks, NE:2 * NE], ALU.add)\
                    .then_inc(sm["acs_set"], 1)

            ln1(0, 0)
            ln1(0, 1)
            prepare()
            y_low(0, 0)
            masks(0)
            for s in range(STAGES):
                if s in W1_TR:
                    for i in range(4):
                        weight(4 * (s - W1_TR[0]) + i)
                attention(0, s)
                if s == 0:
                    split_y(1, 1)
                    weight_scale(0)
                if s == 12:
                    weight_scale(1)
            for g in range(GROUPS):
                group(0, g, 1, w3=True)
            with dve.Fori(0, PAIRS - 2) as i:
                for g in range(GROUPS):
                    group(i + 1, g, i + 2)
            for g in range(GROUPS - 1):
                group(PAIRS - 1, g)
            last_sums(0)
            ffn(PAIRS - 1, GROUPS - 1)
            last_sums(1)
            dve.wait_ge(sm["row_in"], 16)
            dve.wait_ge(sm["fs_set"], 2)
            for h in range(2):
                dve.wait_ge(sm["fin_mm"], h + 1)
                at = slice(512 * h, 512 * h + 512)
                dve.scalar_tensor_tensor(out=out8[:, at], in0=att[h][0:NE, :], scalar=fs[0:NE, 3:4], in1=wrs[:, at],
                                         op0=ALU.mult, op1=ALU.add).then_inc(sm["fin_ready"], 1)


_INS = {"x": "x", "ctx": "ctx_1024", "mask": "mask_Bx1x2048_ff1", "mask_cond": "mask_Bx1x1024_ff1",
        "g_xattn": "g_xattn", "g_ffn": "g_ffn",
        "wq": "L0_xattn_wq", "bq": "L0_xattn_bq", "wk": "L0_xattn_wk", "bk": "L0_xattn_bk",
        "wv": "L0_xattn_wv", "bv": "L0_xattn_bv", "wo": "L0_xattn_wo", "bo": "L0_xattn_bo",
        "gamma": "L0_xattn_gamma", "beta": "L0_xattn_beta",
        "w1": "L0_ffn_w1", "w3": "L0_ffn_w3", "w2": "L0_ffn_w2", "wr": "L0_ffn_wr"}


def kernel(**inputs):
    import numpy as _np
    import concourse.bacc as _bacc
    from concourse import mybir as _mybir
    from concourse.bass_utils import run_bass_kernel_spmd as _run

    nc = _bacc.Bacc("TRN2", target_bir_lowering=False, num_devices=1)
    arrays, aps = {}, {}
    for short, name in _INS.items():
        v = _np.ascontiguousarray(inputs[name])
        arrays[f"in_{short}_dram"] = v
        aps[short] = nc.dram_tensor(f"in_{short}_dram", v.shape, _mybir.dt.from_np(v.dtype), kind="ExternalInput").ap()
    out = nc.dram_tensor("out_0_dram", (NB, S, T), _mybir.dt.from_np(_np.dtype("float32")), kind="ExternalOutput").ap()
    build(nc, aps, out)
    r = _run(nc, [arrays], core_ids=[0])
    return r.results[0]["out_0_dram"]
```
